# Optimizing a Trainium2 kernel written in Bass

```python
import numpy as np
import jax
import jax.numpy as jnp

def _softmax(x, axis=-1):
    return jax.nn.softmax(x, axis=axis)

def _gelu(x):
    return jax.nn.gelu(x, approximate=True)

def _silu(x):
    return jax.nn.silu(x)

def _sigmoid(x):
    return jax.nn.sigmoid(x)

def _layernorm(x, axis=-1, eps=1e-05):
    m = jnp.mean(x, axis=axis, keepdims=True)
    v = jnp.var(x, axis=axis, keepdims=True)
    return (x - m) / jnp.sqrt(v + eps)

def _scatter_add(tgt, idx, src, axis=0):
    return tgt.at[idx].add(src)

def _segment_sum(src, seg, n):
    return jax.ops.segment_sum(src, seg, n)
kernel_name = 'mk_conv_seq_d1_conv_nhwc256_r4_6969c6'

def setup_inputs(seed: int=0):
    np.random.seed(seed)
    _w = jnp.asarray

    def _rec_inputs():
        import jax
        import jax.numpy as jnp
        _gk = jax.random.key(seed)
        x = -0.0003957 + 1 * jax.random.normal(jax.random.fold_in(_gk, 1), (16, 56, 56, 64), jnp.float32)
        return x
    x = _rec_inputs()

    def _L0_conv_setup():
        import jax, jax.numpy as jnp
        import numpy as np
        from jax import lax
        B, H, W, C = (16, 56, 56, 64)
        NH = 8
        KD = C // NH
        FF = 256
        EPS = 1e-06
        SCALE = KD ** (-0.5)

        def _layernorm(x, g, b):
            m = jnp.mean(x, axis=-1, keepdims=True)
            v = jnp.mean(jnp.square(x - m), axis=-1, keepdims=True)
            return (x - m) * lax.rsqrt(v + EPS) * g + b

        def _dwconv(x, w, b):
            return lax.conv_general_dilated(x, w, window_strides=(1, 1), padding='SAME', dimension_numbers=('NHWC', 'HWIO', 'NHWC'), feature_group_count=x.shape[-1]) + b

        def _masa(x, mask_h, mask_w, q_w, q_b, k_w, k_b, v_w, v_b, lepe_w, lepe_b, out_w, out_b):
            b, h, w, _ = x.shape
            q = x @ q_w + q_b
            k = (x @ k_w + k_b) * SCALE
            v = x @ v_w + v_b
            lepe = _dwconv(v, lepe_w, lepe_b)
            qh = q.reshape(b, h, w, NH, KD)
            kh = k.reshape(b, h, w, NH, KD)
            vh = v.reshape(b, h, w, NH, KD)
            attn_w = jax.nn.softmax(jnp.einsum('bhqnd,bhknd->bhnqk', qh, kh) + mask_w, axis=-1)
            vw = jnp.einsum('bhnqk,bhknd->bhnqd', attn_w, vh)
            attn_h = jax.nn.softmax(jnp.einsum('bqwnd,bkwnd->bwnqk', qh, kh) + mask_h, axis=-1)
            out = jnp.einsum('bwnqk,bknwd->bqwnd', attn_h, vw)
            out = out.reshape(b, h, w, NH * KD) + lepe
            return out @ out_w + out_b
        key = jax.random.key(seed)
        ks = jax.random.split(key, 20)
        r = lambda i, shape, s=0.02: jax.random.normal(ks[i], shape, jnp.float32) * s
        return {'x': jax.random.normal(ks[0], (B, H, W, C), jnp.float32), 'mask_h': jax.random.normal(ks[1], (NH, H, H), jnp.float32), 'mask_w': jax.random.normal(ks[2], (NH, W, W), jnp.float32), 'pos_w': r(3, (3, 3, 1, C)), 'pos_b': jnp.zeros((C,), jnp.float32), 'ln1_g': jnp.ones((C,), jnp.float32), 'ln1_b': jnp.zeros((C,), jnp.float32), 'q_w': r(4, (C, C)), 'q_b': jnp.zeros((C,), jnp.float32), 'k_w': r(5, (C, C)), 'k_b': jnp.zeros((C,), jnp.float32), 'v_w': r(6, (C, C)), 'v_b': jnp.zeros((C,), jnp.float32), 'lepe_w': r(7, (5, 5, 1, C)), 'lepe_b': jnp.zeros((C,), jnp.float32), 'out_w': r(8, (C, C)), 'out_b': jnp.zeros((C,), jnp.float32), 'ln2_g': jnp.ones((C,), jnp.float32), 'ln2_b': jnp.zeros((C,), jnp.float32), 'fc1_w': r(9, (C, FF)), 'fc1_b': jnp.zeros((FF,), jnp.float32), 'fc2_w': r(10, (FF, C)), 'fc2_b': jnp.zeros((C,), jnp.float32)}
    _L0_conv_all = _L0_conv_setup()
    _L0_conv_in = {k: v for k, v in _L0_conv_all.items() if k in ('mask_h', 'mask_w', 'pos_w', 'pos_b', 'ln1_g', 'ln1_b', 'q_w', 'q_b', 'k_w', 'k_b', 'v_w', 'v_b', 'lepe_w', 'lepe_b', 'out_w', 'out_b', 'ln2_g', 'ln2_b', 'fc1_w', 'fc1_b', 'fc2_w', 'fc2_b')}
    del _L0_conv_all
    return {'x': x, 'L0_conv_mask_h': _L0_conv_in['mask_h'], 'L0_conv_mask_w': _L0_conv_in['mask_w'], 'L0_conv_pos_w': _L0_conv_in['pos_w'], 'L0_conv_pos_b': _L0_conv_in['pos_b'], 'L0_conv_ln1_g': _L0_conv_in['ln1_g'], 'L0_conv_ln1_b': _L0_conv_in['ln1_b'], 'L0_conv_q_w': _L0_conv_in['q_w'], 'L0_conv_q_b': _L0_conv_in['q_b'], 'L0_conv_k_w': _L0_conv_in['k_w'], 'L0_conv_k_b': _L0_conv_in['k_b'], 'L0_conv_v_w': _L0_conv_in['v_w'], 'L0_conv_v_b': _L0_conv_in['v_b'], 'L0_conv_lepe_w': _L0_conv_in['lepe_w'], 'L0_conv_lepe_b': _L0_conv_in['lepe_b'], 'L0_conv_out_w': _L0_conv_in['out_w'], 'L0_conv_out_b': _L0_conv_in['out_b'], 'L0_conv_ln2_g': _L0_conv_in['ln2_g'], 'L0_conv_ln2_b': _L0_conv_in['ln2_b'], 'L0_conv_fc1_w': _L0_conv_in['fc1_w'], 'L0_conv_fc1_b': _L0_conv_in['fc1_b'], 'L0_conv_fc2_w': _L0_conv_in['fc2_w'], 'L0_conv_fc2_b': _L0_conv_in['fc2_b']}

def reference(x, L0_conv_mask_h, L0_conv_mask_w, L0_conv_pos_w, L0_conv_pos_b, L0_conv_ln1_g, L0_conv_ln1_b, L0_conv_q_w, L0_conv_q_b, L0_conv_k_w, L0_conv_k_b, L0_conv_v_w, L0_conv_v_b, L0_conv_lepe_w, L0_conv_lepe_b, L0_conv_out_w, L0_conv_out_b, L0_conv_ln2_g, L0_conv_ln2_b, L0_conv_fc1_w, L0_conv_fc1_b, L0_conv_fc2_w, L0_conv_fc2_b):
    import jax
    import jax.numpy as jnp

    def _L0_conv_ref(x, mask_h, mask_w, pos_w, pos_b, ln1_g, ln1_b, q_w, q_b, k_w, k_b, v_w, v_b, lepe_w, lepe_b, out_w, out_b, ln2_g, ln2_b, fc1_w, fc1_b, fc2_w, fc2_b):
        import jax, jax.numpy as jnp
        import numpy as np
        from jax import lax
        B, H, W, C = (16, 56, 56, 64)
        NH = 8
        KD = C // NH
        FF = 256
        EPS = 1e-06
        SCALE = KD ** (-0.5)

        def _layernorm(x, g, b):
            m = jnp.mean(x, axis=-1, keepdims=True)
            v = jnp.mean(jnp.square(x - m), axis=-1, keepdims=True)
            return (x - m) * lax.rsqrt(v + EPS) * g + b

        def _dwconv(x, w, b):
            return lax.conv_general_dilated(x, w, window_strides=(1, 1), padding='SAME', dimension_numbers=('NHWC', 'HWIO', 'NHWC'), feature_group_count=x.shape[-1]) + b

        def _masa(x, mask_h, mask_w, q_w, q_b, k_w, k_b, v_w, v_b, lepe_w, lepe_b, out_w, out_b):
            b, h, w, _ = x.shape
            q = x @ q_w + q_b
            k = (x @ k_w + k_b) * SCALE
            v = x @ v_w + v_b
            lepe = _dwconv(v, lepe_w, lepe_b)
            qh = q.reshape(b, h, w, NH, KD)
            kh = k.reshape(b, h, w, NH, KD)
            vh = v.reshape(b, h, w, NH, KD)
            attn_w = jax.nn.softmax(jnp.einsum('bhqnd,bhknd->bhnqk', qh, kh) + mask_w, axis=-1)
            vw = jnp.einsum('bhnqk,bhknd->bhnqd', attn_w, vh)
            attn_h = jax.nn.softmax(jnp.einsum('bqwnd,bkwnd->bwnqk', qh, kh) + mask_h, axis=-1)
            out = jnp.einsum('bwnqk,bknwd->bqwnd', attn_h, vw)
            out = out.reshape(b, h, w, NH * KD) + lepe
            return out @ out_w + out_b
        x = x + _dwconv(x, pos_w, pos_b)
        x = x + _masa(_layernorm(x, ln1_g, ln1_b), mask_h, mask_w, q_w, q_b, k_w, k_b, v_w, v_b, lepe_w, lepe_b, out_w, out_b)
        y = _layernorm(x, ln2_g, ln2_b)
        y = jax.nn.gelu(y @ fc1_w + fc1_b, approximate=False) @ fc2_w + fc2_b
        return x + y

    def _gn(v, G=32, eps=1e-05):
        B_, H_, W_, C_ = v.shape
        g = v.reshape(B_, H_, W_, G, C_ // G)
        m = jnp.mean(g, axis=(1, 2, 4), keepdims=True)
        s = jnp.var(g, axis=(1, 2, 4), keepdims=True)
        return ((g - m) / jnp.sqrt(s + eps)).reshape(v.shape)

    def _ln_c(v, eps=1e-06):
        m = jnp.mean(v, axis=-1, keepdims=True)
        s = jnp.var(v, axis=-1, keepdims=True)
        return (v - m) / jnp.sqrt(s + eps)

    def _ln_t(v, eps=1e-05):
        m = jnp.mean(v, axis=-1, keepdims=True)
        s = jnp.var(v, axis=-1, keepdims=True)
        return (v - m) / jnp.sqrt(s + eps)

    def _to_tokens(v):
        B_, H_, W_, C_ = v.shape
        return v.reshape(B_, H_ * W_, C_)

    def _from_tokens(t, like):
        return t.reshape(like.shape)
    x = _L0_conv_ref(x, L0_conv_mask_h, L0_conv_mask_w, L0_conv_pos_w, L0_conv_pos_b, L0_conv_ln1_g, L0_conv_ln1_b, L0_conv_q_w, L0_conv_q_b, L0_conv_k_w, L0_conv_k_b, L0_conv_v_w, L0_conv_v_b, L0_conv_lepe_w, L0_conv_lepe_b, L0_conv_out_w, L0_conv_out_b, L0_conv_ln2_g, L0_conv_ln2_b, L0_conv_fc1_w, L0_conv_fc1_b, L0_conv_fc2_w, L0_conv_fc2_b)
    return x

_drawn_inputs = setup_inputs


def setup_inputs(seed=0):
    import zlib

    import numpy as np

    out = dict(_drawn_inputs(seed))
    spreads = {'L0_conv_pos_b': (0.0, 0.1),
     'L0_conv_ln1_g': (1.0, 0.6),
     'L0_conv_ln1_b': (0.0, 0.8),
     'L0_conv_q_b': (0.0, 0.8),
     'L0_conv_k_b': (0.0, 2.0),
     'L0_conv_v_b': (0.0, 0.542),
     'L0_conv_lepe_b': (0.0, 0.452),
     'L0_conv_out_b': (0.0, 0.1),
     'L0_conv_ln2_g': (1.0, 0.6),
     'L0_conv_ln2_b': (0.0, 2.0),
     'L0_conv_fc1_b': (0.0, 0.445),
     'L0_conv_fc2_b': (0.0, 0.1)}
    factors = {'L0_conv_mask_h': 8.0,
     'L0_conv_mask_w': 8.0,
     'L0_conv_q_w': 8.0,
     'L0_conv_k_w': 8.0,
     'L0_conv_v_w': 8.0,
     'L0_conv_lepe_w': 8.0}
    for name, (base, spread) in spreads.items():
        noise = np.random.default_rng([zlib.crc32(name.encode()), seed]).standard_normal(out[name].shape)
        drawn = base * np.exp(spread * noise) if base else spread * noise
        out[name] = jnp.asarray(drawn.astype(out[name].dtype))
    for name, factor in factors.items():
        out[name] = (out[name] * factor).astype(out[name].dtype)
    return out
```

```python
from contextlib import ExitStack

import concourse.bass as bass
from concourse import mybir

F32 = mybir.dt.float32
BF16 = mybir.dt.bfloat16
ALU = mybir.AluOpType
ACT = mybir.ActivationFunctionType
AX = mybir.AxisListType

B, H, W, C = 16, 56, 56, 64
NH, KD, FF = 8, 8, 256
EPS = 1e-6
SCALE = KD ** -0.5
L = 56
LINES = 14
PAIRS = LINES // 2
G = H // LINES
NCH = B * G
CW = LINES * L
HALF = CW // 2
S8 = NH * L
R1 = 64
VW = 4 * 36
TAIL = 60


class Alloc:

    def __init__(self, nc, ctx, tag):
        self.nc, self.ctx, self.tag, self.sems = nc, ctx, tag, []
        ctx.callback(self.close)

    def close(self):
        self.nc.all_engine_barrier()
        self.nc.clear_and_free_semaphores(self.sems)
        self.nc.all_engine_barrier()

    def sb(self, name, shape, dt):
        return self.ctx.enter_context(self.nc.sbuf_tensor(f"{self.tag}_{name}", shape, dt))

    def ps(self, name, shape, dt):
        return self.ctx.enter_context(self.nc.psum_tensor(f"{self.tag}_{name}", shape, dt))

    def sem(self, name):
        self.sems.append(self.nc.alloc_semaphore(f"{self.tag}_{name}"))
        return self.sems[-1]


def identity_on(pool, ident, zeroed, made):
    pool.memset(ident[:, :], 0.0).then_inc(zeroed, 1)
    pool.wait_ge(zeroed, 1)
    pool.affine_select(out=ident[:, :], in_=ident[:, :], compare_op=ALU.not_equal, fill=1.0, base=0,
                       pattern=[[-1, 128]], channel_multiplier=1).then_inc(made, 1)


def attention_phase(nc, tag, rows, xt_d, mask_d, w_d, b_d, ln_g, ln_b, v_d, out_d):
    with ExitStack() as ctx:
        al = Alloc(nc, ctx, tag)
        sb, sem = al.sb, al.sem
        xt = [sb(f"xt{u}", [128, CW], BF16) for u in range(2)]
        k_hilo = [sb(f"k_hilo{v}", [128, CW], BF16) for v in range(4)]
        k_unit = [sb(f"k_unit{v}", [128, CW], BF16) for v in range(4)]
        q_unit = [sb(f"q_unit{u}", [128, CW], BF16) for u in range(2)]
        q_src = [sb(f"q_src{u}", [128, 2, CW], BF16) for u in range(2)]
        kx = [sb(f"kx{u}", [128, NH, CW], BF16) for u in range(2)]
        qx = [sb(f"qx{u}", [128, 2, NH, CW], BF16) for u in range(2)]
        vf = [sb(f"vf{u}", [128, PAIRS * C], F32) for u in range(2)]
        vx = [sb(f"vx{v}", [128, PAIRS * VW + TAIL], F32) for v in range(4)]
        mx = [sb(f"mx{u}", [128, 2, NH, L], BF16) for u in range(2)]
        mm = [sb(f"mm{u}", [128, 128], F32) for u in range(2)]
        prob = [sb(f"prob{t}", [128, NH, 64], F32) for t in range(4)]
        o_sb = [sb(f"o_sb{u}", [128, 2, PAIRS, 32], F32) for u in range(2)]
        rec = [sb(f"rec{u}", [128, 3 * 8], F32) for u in range(2)]
        ident = sb("ident", [128, 128], F32)
        pick = sb("pick", [128, PAIRS, L], BF16)
        negd = sb("negd", [128, NH], F32)
        sel7 = sb("sel7", [128, PAIRS], F32)
        mask_f = sb("mask_f", [128, NH, L], F32)
        mlo_hi = sb("mlo_hi", [128, NH, L], BF16)
        mlo = sb("mlo", [128, NH, L], BF16)
        wf = [sb(f"wf{n}", [128, C], F32) for n in "qkv"]
        wg = [sb(f"wg{n}", [128, C], F32) for n in "qkv"]
        w1 = [sb(f"w1{n}", [128, 2 * C], BF16) for n in "qkv"]
        w2 = [sb(f"w2{n}", [128, 2 * C], BF16) for n in "qkv"]
        wdup = [sb(f"wdup{n}", [C, 2 * C], F32) for n in "qk"]
        g_c = sb("g_c", [128, 1], F32)
        b_c = sb("b_c", [128, 1], F32)
        b_wide = sb("b_wide", [C, 128], F32)
        b_in = sb("b_in", [128, 2], F32)
        bias = sb("bias", [128, 2], F32)
        bv_in = sb("bv_in", [128, C], F32)
        bv = sb("bv", [128, C], F32)

        s_ps = [al.ps(f"s_ps{u}", [128, 512], F32) for u in range(2)]
        st_ps = [al.ps(f"st_ps{u}", [128, 512], F32) for u in range(2)]
        pv_ps = [al.ps(f"pv_ps{u}", [128, 512], F32) for u in range(2)]
        pj = [al.ps(f"pj{u}", [128, 512], F32) for u in range(2)]

        par = sem("par")
        zeroed, unit = sem("zeroed"), sem("unit")
        cleared = sem("cleared")
        prep = sem("prep")
        pre_pe = sem("pre_pe")
        ready = sem("ready")
        xt_in = [sem(f"xt_in{u}") for u in range(2)]
        kx_in = [sem(f"kx_in{u}") for u in range(2)]
        qx_in = [sem(f"qx_in{u}") for u in range(2)]
        kx_in_sw = [sem(f"kx_in_sw{u}") for u in range(2)]
        qx_in_sw = [sem(f"qx_in_sw{u}") for u in range(2)]
        v_io = [sem(f"v_io{u}") for u in range(2)]
        o_out = [sem(f"o_out{u}") for u in range(2)]
        k_proj, q_proj, v_proj = sem("k_proj"), sem("q_proj"), sem("v_proj")
        s_done, mt_done = sem("s_done"), sem("mt_done")
        st_done, pv_done = sem("st_done"), sem("pv_done")
        k_hi, q_hi, exp_done = sem("k_hi"), sem("q_hi"), sem("exp_done")
        k_lo, k_cp = sem("k_lo"), sem("k_cp")
        q_lo, q_cp = sem("q_lo"), sem("q_cp")
        v_sb = sem("v_sb")
        max_done, mx_done = sem("max_done"), sem("mx_done")
        rec_done, norm_done = sem("rec_done"), sem("norm_done")
        vx_done = sem("vx_done")

        def lines(t):
            return (t if isinstance(t, bass.AP) else t[:, :]).rearrange("p (l q) -> p l q", q=L)

        def chunk_tokens(dram, i, v):
            if rows:
                return dram.rearrange("b (g l) q c -> (b g) q l c", l=LINES)[4 * i + v]
            return dram.rearrange("b q (g l) c -> b g q l c", l=LINES)[i, v]

        def loop(eng, body, first):
            first()
            for v in range(4):
                body(0, v, True, True)
            with eng.Fori(1, B - 1) as i:
                for v in range(4):
                    body(i, v, True, True)
            for v in range(4):
                body(B - 1, v, v < 3, v < 2)

        passed = {mybir.EngineType.Pool: sem("passed_pool"), mybir.EngineType.SP: sem("passed_sp")}

        def cnt(i, v, per, plus):
            return i * (4 * per) + (v * per + plus)

        def nxt(i, v, d):
            return (i + 1, v + d - 4) if v + d >= 4 else (i, v + d)

        def wait(eng, s, val):
            if not isinstance(val, int):
                eng.wait_ge(s, val)
                if eng.engine in passed:
                    eng.sem_inc(passed[eng.engine], 1)
            elif val > 0:
                eng.wait_ge(s, val)

        block = ctx.enter_context(nc.Block())

        def fill_k(eng, i, v, slots, sems):
            u = v % 2
            wait(eng, k_cp, cnt(i, v, 1, 1))
            wait(eng, s_done, cnt(i, v, 7, -7))
            for s in slots:
                n = 4 * (s % 2) + s // 2
                eng.dma_start(kx[u][8 * n:8 * n + 8, s, :], k_hilo[v][8 * n:8 * n + 8, :]).then_inc(sems[u], 16)

        def fill_q(eng, i, v, slots, high, sems):
            u = v % 2
            wait(eng, q_cp, cnt(i, v, 1, 1))
            wait(eng, st_done, cnt(i, v, 7, -7))
            for s in slots:
                n = 4 * (s % 2) + s // 2
                eng.dma_start(qx[u][8 * n:8 * n + 8, :, s, :], q_src[u][8 * n:8 * n + 8, :, :]).then_inc(sems[u], 16)
            for s in high:
                n = 4 * (s % 2) + s // 2
                eng.dma_start(qx[u][64 + 8 * n:72 + 8 * n, 1, s, :],
                              q_src[u][64 + 8 * n:72 + 8 * n, 1, :]).then_inc(sems[u], 16)

        def filled(eng, s, s_sw, i, v, sp_n, pool_n):
            u = v % 2
            for x, n in ((s[u], 16 * sp_n), (s_sw[u], 16 * pool_n)):
                wait(eng, x, i * 2 * n + (v // 2 + 1) * n)

        K_SP, K_POOL = range(0, 5), range(5, 8)
        Q_SP, Q_POOL = (range(0, 5), range(0, 5)), (range(5, 8), range(5, 8))
        NK_SP, NK_POOL = len(K_SP), len(K_POOL)
        NQ_SP, NQ_POOL = sum(map(len, Q_SP)), sum(map(len, Q_POOL))

        @block.sync
        def _(sp):
            def load_x(i, v):
                u = v % 2
                if rows:
                    wait(sp, v_proj, cnt(i, v, 1, -1))
                else:
                    wait(sp, q_proj, cnt(i, v, 2, -2))
                sp.dma_start(xt[u][:, :], xt_d[4 * i + v]).then_inc(xt_in[u], 16)

            def load_v(i, v):
                u = v % 2
                wait(sp, vx_done, cnt(i, v, 4, -4))
                src = chunk_tokens(v_d, i, v)
                for r in range(2):
                    sp.dma_start(vf[u][64 * r:64 * r + L, :].rearrange("p (j c) -> p j c", c=C),
                                 src[:, PAIRS * r:PAIRS * r + PAIRS, :]).then_inc(v_io[u], 16)

            def store_v(i, v):
                u = v % 2
                wait(sp, v_sb, cnt(i, v, 1, 1))
                dst = chunk_tokens(v_d, i, v)
                for r in range(2):
                    sp.dma_start(dst[:, PAIRS * r:PAIRS * r + PAIRS, :],
                                 vf[u][64 * r:64 * r + L, :].rearrange("p (j c) -> p j c", c=C)).then_inc(v_io[u], 16)

            def store_o(i, v):
                u = v % 2
                wait(sp, norm_done, cnt(i, v, 6, 6))
                dst = chunk_tokens(out_d, i, v)
                for h in range(2):
                    sp.dma_start(dst[:, :, 32 * h:32 * h + 32],
                                 o_sb[u][64 * h:64 * h + L].rearrange("p r j c -> p (r j) c")).then_inc(o_out[u], 16)

            def first():
                for n in range(3):
                    for h in range(2):
                        sp.dma_start(wf[n][64 * h:64 * h + 64, :], w_d[n]).then_inc(par, 16)
                    if n < 2:
                        for h in range(2):
                            sp.dma_start(b_in[64 * h:64 * h + 64, n:n + 1], b_d[n].unsqueeze(1)).then_inc(par, 16)
                for h in range(2):
                    sp.dma_start(g_c[64 * h:64 * h + 64, :], ln_g.unsqueeze(1)).then_inc(par, 16)
                    sp.dma_start(b_c[64 * h:64 * h + 64, :], ln_b.unsqueeze(1)).then_inc(par, 16)
                sp.dma_start(bv_in[:, :], b_d[2].partition_broadcast(128)).then_inc(par, 16)
                m = mask_d.rearrange("(i a) q k -> q i a k", i=2)
                for h in range(2):
                    for i in range(2):
                        sp.dma_start(mask_f[64 * h:64 * h + L].rearrange("p (a i) k -> p i a k", i=2)[:, i],
                                     m[:, i]).then_inc(par, 16)
                load_x(0, 0)
                load_x(0, 1)
                if not rows:
                    load_v(0, 0)
                    load_v(0, 1)
                sp.wait_ge(ready, 1)
                fill_k(sp, 0, 0, K_SP, kx_in)
                fill_q(sp, 0, 0, *Q_SP, qx_in)
                fill_k(sp, 0, 1, K_SP, kx_in)
                load_x(0, 2)
                if rows:
                    store_v(0, 0)
                    store_v(0, 1)

            def body(i, v, more_s, more_p):
                if more_s:
                    fill_q(sp, *nxt(i, v, 1), *Q_SP, qx_in)
                if more_p:
                    if not rows:
                        load_v(*nxt(i, v, 2))
                    fill_k(sp, *nxt(i, v, 2), K_SP, kx_in)
                    if not (isinstance(i, int) and i == B - 1 and v >= 1):
                        load_x(*nxt(i, v, 3))
                    if rows:
                        store_v(*nxt(i, v, 2))
                store_o(i, v)

            loop(sp, body, first)
            for u in range(2):
                sp.wait_ge(o_out[u], 32 * (NCH // 2))
                if rows:
                    sp.wait_ge(v_io[u], 32 * (NCH // 2))

        @block.gpsimd
        def _(pool):
            def build_vx(i, v):
                u = v % 2
                if rows:
                    wait(pool, v_sb, cnt(i, v, 1, 1))
                else:
                    wait(pool, v_io[u], i * 64 + (v // 2) * 32 + 32)
                wait(pool, pv_done, cnt(i, v, 7, -21))
                dst = vx[v][:, 0:PAIRS * VW].rearrange("p (j a i r d) -> p j a i r d", a=4, i=2, r=2, d=9)
                src = vf[u][:, :].rearrange("p (j i a d) -> p j a i d", i=2, a=4, d=8)
                for r in range(2):
                    rows_ = slice(64 * r, 64 * r + L)
                    for h in range(2):
                        pool.tensor_copy(dst[rows_, :, :, h, r, 0:8], src[rows_, :, :, h, :]).then_inc(vx_done, 1)

            def first():
                identity_on(pool, ident, zeroed, unit)
                pool.wait_ge(ready, 1)
                build_vx(0, 0)
                fill_k(pool, 0, 0, K_POOL, kx_in_sw)
                fill_q(pool, 0, 0, *Q_POOL, qx_in_sw)
                build_vx(0, 1)
                fill_k(pool, 0, 1, K_POOL, kx_in_sw)

            def body(i, v, more_s, more_p):
                if more_s:
                    fill_q(pool, *nxt(i, v, 1), *Q_POOL, qx_in_sw)
                if more_p:
                    fill_k(pool, *nxt(i, v, 2), K_POOL, kx_in_sw)
                    build_vx(*nxt(i, v, 2))

            loop(pool, body, first)

        @block.tensor
        def _(pe):
            def project(i, v, n, done, free):
                u = v % 2
                for h in range(2):
                    cols = slice(HALF * h, HALF * h + HALF)
                    for s, val in free(h):
                        wait(pe, s, val)
                    pe.matmul(pj[h][:, 0:HALF], w1[n][:, :], xt[u][:, cols], start=True, stop=False)
                    pe.matmul(pj[h][:, 0:HALF], w2[n][:, :], xt[u][:, cols], start=False, stop=True).then_inc(done, 1)

            def project_k(i, v):
                pe.wait_ge(xt_in[v % 2], i * 32 + (v // 2) * 16 + 16)
                if rows:
                    project(i, v, 1, k_proj, lambda h: [(v_sb, cnt(i, v, 1, 0))] if h == 0 else
                            [(q_lo, cnt(i, v, 2, 0))])
                else:
                    project(i, v, 1, k_proj, lambda h: [(q_lo, cnt(i, v, 2, h - 1))])

            def project_q(i, v):
                project(i, v, 0, q_proj, lambda h: [(k_lo, cnt(i, v, 2, h + 1))])

            def project_v(i, v):
                wait(pe, q_lo, cnt(i, v, 2, 1))
                x = lines(xt[v % 2])
                for j in range(PAIRS):
                    for part, w in enumerate((w1[2], w2[2])):
                        for r in range(2):
                            ins = pe.matmul(pj[0][64 * r:64 * r + L, C * j:C * j + C], x[:, PAIRS * r + j, :],
                                            w[:, 0:C], start=part == 0, stop=part == 1)
                ins.then_inc(v_proj, 1)

            def scores(i, v, j):
                u = v % 2
                if j == 0:
                    filled(pe, kx_in, kx_in_sw, i, v, NK_SP, NK_POOL)
                    wait(pe, q_cp, cnt(i, v, 1, 1))
                if j == 1:
                    wait(pe, mx_done, cnt(i, v, 2, 0))
                else:
                    wait(pe, max_done, cnt(i, v, 7, j - 1 if j else 0))
                q, k = lines(q_unit[u]), kx[u][:, :, :].rearrange("p s (l q) -> p s l q", q=L)
                for r in range(2):
                    ins = pe.matmul(s_ps[j % 2][64 * r:64 * r + L, 0:S8].rearrange("p (s k) -> p s k", k=L),
                                    q[0:120, PAIRS * r + j, :], k[0:120, :, PAIRS * r + j, :],
                                    start=True, stop=True)
                ins.then_inc(s_done, 1)

            def maxima(i, v):
                pe.wait_ge(max_done, cnt(i, v, 7, 7))
                pe.transpose(s_ps[1][0:120, 0:128], mm[v % 2][:, 0:120], ident[:, :]).then_inc(mt_done, 1)

            def scores_t(i, v, j):
                u, t = v % 2, 7 * v + j
                if j == 0:
                    filled(pe, qx_in, qx_in_sw, i, v, NQ_SP, NQ_POOL)
                    pe.wait_ge(mx_done, cnt(i, v, 2, 2))
                wait(pe, exp_done, i * 28 + t - 1)
                kh, ku = lines(k_hilo[v]), lines(k_unit[v])
                q = qx[u][:, :, :, :].rearrange("p t s (l q) -> p t s l q", q=L)
                out = st_ps[t % 2][:, 0:S8].rearrange("p (s q) -> p s q", q=L)
                for n in range(3):
                    for r in range(2):
                        ln = PAIRS * r + j
                        lhs, rhs = ((kh[:, ln, :], q[:, 1, :, ln, :]),
                                    (ku[0:120, ln, :], q[0:120, 0, :, ln, :]),
                                    (pick[0:120, j, :], mx[u][0:120, r, :, :]))[n]
                        ins = pe.matmul(out[64 * r:64 * r + L], lhs, rhs, start=n == 0, stop=n == 2)
                ins.then_inc(st_done, 1)

            def products(i, v, j):
                t, g = 7 * v + j, 3 * v + j // 3
                if j == 0:
                    pe.wait_ge(vx_done, cnt(i, v, 4, 4))
                if j % 3 == 0:
                    wait(pe, norm_done, i * 24 + 2 * g - 2)
                pe.wait_ge(exp_done, i * 28 + t + 1)
                for a in range(4):
                    at = VW * (j % 3) + 36 * a
                    ins = pe.matmul(pv_ps[g % 2][0:120, at:at + 96],
                                    prob[t % 4][:, 2 * a:2 * a + 2, :].rearrange("p i q -> p (i q)")[:, 0:120],
                                    vx[v][:, VW * j + 36 * a:VW * j + 36 * a + 96], start=True, stop=True)
                ins.then_inc(pv_done, 1)

            def first():
                pe.wait_ge(par, 16 * 19)
                pe.wait_ge(unit, 1)
                pe.wait_ge(cleared, 1)
                for h in range(2):
                    for s in range(NH):
                        ins = pe.matmul(s_ps[0][64 * h:64 * h + L, L * s:L * s + L], mask_f[0:L, s, :],
                                        ident[0:L, 0:L], start=True, stop=True)
                ins.then_inc(pre_pe, 1)
                pe.wait_ge(prep, 2)
                for n in range(2):
                    pe.matmul(s_ps[1][:, n:n + 1], wdup[n][:, :], b_c[0:C, :], start=True, stop=True)
                pe.matmul(s_ps[1][:, C:2 * C], b_wide[:, :], wf[2][0:C, :], start=True, stop=True).then_inc(pre_pe, 1)
                pe.wait_ge(ready, 1)
                for v in range(2):
                    project_k(0, v)
                    project_q(0, v)
                    if rows:
                        project_v(0, v)
                for j in range(PAIRS):
                    scores(0, 0, j)
                maxima(0, 0)

            def body(i, v, more_s, more_p):
                n1, n2 = nxt(i, v, 1), nxt(i, v, 2)
                for j in range(PAIRS):
                    scores_t(i, v, j)
                    if j:
                        products(i, v, j - 1)
                    elif not (isinstance(i, int) and i == 0 and v == 0):
                        products(*nxt(i, v, -1) if v else (i - 1, 3), PAIRS - 1)
                    if more_p and j == 0:
                        project_k(*n2)
                    if more_s:
                        if j == 0:
                            scores(*n1, 0)
                        if j < PAIRS - 1:
                            scores(*n1, j + 1)
                        else:
                            maxima(*n1)
                    if more_p and j == 1:
                        project_q(*n2)
                    if rows and more_p and j == 3:
                        project_v(*n2)

            loop(pe, body, first)
            products(B - 1, 3, PAIRS - 1)

        @block.scalar
        def _(act):
            def high_k(i, v):
                wait(act, s_done, cnt(i, v, 7, -21))
                wait(act, st_done, cnt(i, v, 7, -21))
                for h in range(2):
                    cols = slice(HALF * h, HALF * h + HALF)
                    act.wait_ge(k_proj, cnt(i, v, 2, h + 1))
                    act.activation(k_hilo[v][:, cols], pj[h][:, 0:HALF], ACT.Identity,
                                   bias=bias[:, 1:2]).then_inc(k_hi, 1)

            def high_q(i, v):
                u = v % 2
                if isinstance(i, int) and i == 0 and v < 2:
                    pass
                elif v < 2:
                    filled(act, qx_in, qx_in_sw, i - 1, v + 2, NQ_SP, NQ_POOL)
                else:
                    filled(act, qx_in, qx_in_sw, i, v - 2, NQ_SP, NQ_POOL)
                for h in range(2):
                    cols = slice(HALF * h, HALF * h + HALF)
                    act.wait_ge(q_proj, cnt(i, v, 2, h + 1))
                    act.activation(q_src[u][:, 1, cols], pj[h][:, 0:HALF], ACT.Identity,
                                   bias=bias[:, 0:1]).then_inc(q_hi, 1)

            def exps(i, v, j):
                t = 7 * v + j
                act.wait_ge(st_done, i * 28 + t + 1)
                wait(act, pv_done, i * 28 + t - 3)
                act.activation(prob[t % 4][:, :, 0:L], st_ps[t % 2][:, 0:S8].rearrange("p (s q) -> p s q", q=L),
                               ACT.Exp).then_inc(exp_done, 1)

            def first():
                act.wait_ge(ready, 1)
                for v in range(2):
                    high_k(0, v)
                    high_q(0, v)

            def body(i, v, more_s, more_p):
                n2 = nxt(i, v, 2)
                for j in range(PAIRS):
                    exps(i, v, j)
                    if more_p and j == 0:
                        high_k(*n2)
                    if more_p and j == 1:
                        high_q(*n2)

            loop(act, body, first)

        @block.vector
        def _(dve):
            def low_k(i, v):
                for h in range(2):
                    cols = slice(HALF * h, HALF * h + HALF)
                    dve.wait_ge(k_hi, cnt(i, v, 2, h + 1))
                    dve.scalar_tensor_tensor(k_hilo[v][64:128, cols], pj[h][64:128, 0:HALF], bias[64:128, 1:2],
                                             k_hilo[v][64:128, cols], ALU.add, ALU.subtract).then_inc(k_lo, 1)
                dve.tensor_copy(k_unit[v][0:64, :], k_hilo[v][0:64, :]).then_inc(k_cp, 1)

            def low_q(i, v):
                u = v % 2
                for h in range(2):
                    cols = slice(HALF * h, HALF * h + HALF)
                    dve.wait_ge(q_hi, cnt(i, v, 2, h + 1))
                    dve.scalar_tensor_tensor(q_src[u][0:64, 0, cols], pj[h][0:64, 0:HALF], bias[0:64, 0:1],
                                             q_src[u][0:64, 1, cols], ALU.add, ALU.subtract).then_inc(q_lo, 1)
                wait(dve, q_lo, cnt(i, v, 2, 2))
                wait(dve, s_done, cnt(i, v, 7, -7))
                dve.tensor_copy(q_unit[u][0:64, :], q_src[u][0:64, 1, :]).then_inc(q_cp, 1)

            def values(i, v):
                u = v % 2
                wait(dve, vx_done, cnt(i, v, 4, -4))
                if isinstance(i, int):
                    wait(dve, v_io[u], i * 64 + (v // 2) * 32)
                else:
                    dve.wait_ge(v_io[u], i * 64 + (v // 2) * 32)
                dve.wait_ge(v_proj, cnt(i, v, 1, 1))
                dve.tensor_tensor(vf[u][:, :].rearrange("p (j c) -> p j c", c=C),
                                  pj[0][:, 0:PAIRS * C].rearrange("p (j c) -> p j c", c=C),
                                  bv[:, :].unsqueeze(1).to_broadcast([128, PAIRS, C]), ALU.add).then_inc(v_sb, 1)

            def line_max(i, v, j):
                dve.wait_ge(s_done, cnt(i, v, 7, j + 1))
                if j == 0:
                    wait(dve, mt_done, cnt(i, v, 1, -1))
                dve.tensor_reduce(mm[v % 2][:, 64 + NH * j:72 + NH * j],
                                  s_ps[j % 2][:, 0:S8].rearrange("p (s k) -> p s k", k=L),
                                  AX.X, ALU.max).then_inc(max_done, 1)

            def spread_max(i, v):
                u = v % 2
                dve.wait_ge(mt_done, cnt(i, v, 1, 1))
                wait(dve, st_done, cnt(i, v, 7, -7))
                for r in range(2):
                    dve.tensor_tensor(mx[u][64:120, r, :, :],
                                      s_ps[1][64:120, 64 * r:64 * r + L].unsqueeze(1).to_broadcast([56, NH, L]),
                                      negd[64:120, :].unsqueeze(2).to_broadcast([56, NH, L]),
                                      ALU.mult).then_inc(mx_done, 1)

            def normalise(i, v, g):
                u, n = v % 2, min(3, PAIRS - 3 * g)
                b = (3 * v + g) % 2
                dve.wait_ge(pv_done, cnt(i, v, 7, 3 * g + n))
                if g == 0:
                    if isinstance(i, int):
                        wait(dve, o_out[u], i * 64 + (v // 2) * 32)
                    else:
                        dve.wait_ge(o_out[u], i * 64 + (v // 2) * 32)
                if g == 0:
                    wait(dve, norm_done, cnt(i, v, 6, 0))
                else:
                    wait(dve, norm_done, cnt(i, v, 6, 2 * g))
                o = o_sb[u][:, :, :, :].rearrange("p r j (a d) -> p (j a) r d", a=4)
                for h in range(2):
                    p = slice(64 * h, 64 * h + L)
                    got = pv_ps[b][p, 0:VW * n].rearrange("p (j i r d) -> p j i r d", i=2, r=2, d=9)[:, :, h]
                    sums = rec[b][p, 0:8 * n].rearrange("p (j r) -> p j r", r=2)
                    dve.reciprocal(sums, got[:, :, :, 8]).then_inc(rec_done, 1)
                for h in range(2):
                    p = slice(64 * h, 64 * h + L)
                    got = pv_ps[b][p, 0:VW * n].rearrange("p (j i r d) -> p j i r d", i=2, r=2, d=9)[:, :, h]
                    sums = rec[b][p, 0:8 * n].rearrange("p (j r) -> p j r", r=2)
                    dve.wait_ge(rec_done, i * 24 + (6 * v + 2 * g + h + 1))
                    dve.tensor_tensor(o[p, 12 * g:12 * g + 4 * n], got[:, :, :, 0:8],
                                      sums.unsqueeze(3).to_broadcast([L, 4 * n, 2, 8]), ALU.mult).then_inc(norm_done, 1)

            def first():
                for t in (*kx, *qx, *vx, *mx, *mm, *prob, *s_ps, *st_ps, *pv_ps, *pj, pick, *w2, *k_unit, *q_unit):
                    nd = len(t.shape)
                    a = t[(slice(None),) * nd]
                    if nd == 3:
                        a = a.rearrange("p a b -> p (a b)")
                    if nd == 4:
                        a = a.rearrange("p a b c -> p (a b c)")
                    if a.dtype == BF16:
                        a = a.bitcast(F32)
                    ins = dve.memset(a, 0.0)
                ins.then_inc(cleared, 1)
                dve.wait_ge(cleared, 1)
                dve.wait_ge(par, 16 * 19)
                dve.wait_ge(unit, 1)
                step = [0]

                def done(ins):
                    step[0] += 1
                    ins.then_inc(prep, 1)

                def settled():
                    dve.wait_ge(prep, step[0])

                for n in range(2):
                    ins = dve.tensor_copy(wdup[n][:, :].rearrange("p (h c) -> p h c", h=2),
                                          wf[n][0:C, :].unsqueeze(1).to_broadcast([C, 2, C]))
                done(ins)
                done(dve.tensor_copy(b_wide[:, :], b_c[0:C, :].to_broadcast([C, 128])))
                for n in range(3):
                    done(dve.tensor_scalar(wg[n][:, :], wf[n][:, :], g_c[:, 0:1], SCALE if n == 1 else 1.0,
                                           ALU.mult, ALU.mult))
                settled()
                for n in range(3):
                    done(dve.tensor_copy(w1[n][:, :].rearrange("p (h c) -> p h c", h=2),
                                         wg[n][:, :].unsqueeze(1).to_broadcast([128, 2, C])))
                settled()
                for n in range(3):
                    done(dve.tensor_tensor(w2[n][0:64, :].rearrange("p (h c) -> p h c", h=2),
                                           wg[n][0:64, :].unsqueeze(1).to_broadcast([64, 2, C]),
                                           w1[n][0:64, :].rearrange("p (h c) -> p h c", h=2), ALU.subtract))
                for v in range(4):
                    d = vx[v][:, 0:PAIRS * VW].rearrange("p (j r d) -> p j r d", r=2, d=9)
                    for r in range(2):
                        done(dve.memset(d[64 * r:64 * r + L, :, r, 8:9], 1.0))
                eye = ident[64:120, 64:120]
                for t in (*k_unit, *q_unit):
                    done(dve.tensor_copy(lines(t)[64:120], eye.unsqueeze(1).to_broadcast([56, LINES, L])))
                done(dve.tensor_copy(pick[0:L], ident[0:L, 0:L].unsqueeze(1).to_broadcast([L, PAIRS, L])))
                done(dve.tensor_reduce(sel7[64:120, :], eye.rearrange("p (j s) -> p j s", s=NH), AX.X, ALU.add))
                done(dve.tensor_reduce(negd[64:120, :], eye.rearrange("p (j s) -> p s j", s=NH), AX.X, ALU.add,
                                       negate=True))
                settled()
                done(dve.tensor_copy(pick[64:120], sel7[64:120, :].unsqueeze(2).to_broadcast([56, PAIRS, L])))
                for u in range(2):
                    for s in range(NH):
                        done(dve.tensor_copy(lines(kx[u][64:120, s, :]),
                                             mask_f[64:120, s:s + 1, :].to_broadcast([56, LINES, L])))
                dve.wait_ge(pre_pe, 1)
                mt = s_ps[0][:, 0:S8].rearrange("p (s q) -> p s q", q=L)
                for u in range(2):
                    for r in range(2):
                        done(dve.tensor_copy(mx[u][0:L, r, :, :], mt[0:L]))
                done(dve.tensor_copy(mlo_hi[64:120], mt[64:120]))
                settled()
                done(dve.tensor_tensor(mlo[64:120], mt[64:120], mlo_hi[64:120], ALU.subtract))
                settled()
                for u in range(2):
                    for s in range(NH):
                        done(dve.tensor_copy(lines(qx[u][64:120, 0, s, :]),
                                             mlo[64:120, s:s + 1, :].to_broadcast([56, LINES, L])))
                dve.wait_ge(pre_pe, 2)
                done(dve.tensor_tensor(bias[:, :], s_ps[1][:, 0:2], b_in[:, :], ALU.add))
                done(dve.tensor_tensor(bv[:, :], s_ps[1][:, C:2 * C], bv_in[:, :], ALU.add))
                settled()
                done(dve.tensor_scalar(bias[:, 1:2], bias[:, 1:2], SCALE, None, ALU.mult))
                settled()
                dve.sem_inc(ready, 1)
                for v in range(2):
                    low_k(0, v)
                    low_q(0, v)
                    if rows:
                        values(0, v)
                for j in range(PAIRS):
                    line_max(0, 0, j)
                spread_max(0, 0)

            def body(i, v, more_s, more_p):
                n1, n2 = nxt(i, v, 1), nxt(i, v, 2)
                for j in range(PAIRS):
                    if j == 0 and not (isinstance(i, int) and i == 0 and v == 0):
                        normalise(*(nxt(i, v, -1) if v else (i - 1, 3)), 2)
                    if more_s and j == 0:
                        line_max(*n1, 0)
                    if more_p and j == 0:
                        low_k(*n2)
                    if more_s:
                        if j < PAIRS - 1:
                            line_max(*n1, j + 1)
                        else:
                            spread_max(*n1)
                    if more_p and j == 1:
                        low_q(*n2)
                    if j == 3:
                        normalise(i, v, 0)
                        if rows and more_p:
                            values(*n2)
                    if j == 6:
                        normalise(i, v, 1)

            loop(dve, body, first)
            normalise(B - 1, 3, 2)


NB4 = 4
NBATCH = B // NB4
J = H // 2
P2 = 2 * W


def conv_phase(nc, tag, pos, src_d, taps_d, bias_d, add_d, mirror_d, band_d, x1_d, xr_d, xc_d):
    R = 1 if pos else 2
    D = 2 * R + 1
    BAND = W + 2 * R
    with ExitStack() as ctx:
        al = Alloc(nc, ctx, tag)
        sb, sem = al.sb, al.sem
        T = sb("taps", [128, 3, P2, C], F32)
        X = [sb(f"x{u}", [128, NB4, J + 2, C], F32) for u in range(2)]
        hl = [sb(f"hl{u}", [P2, J, 2 * C], BF16) for u in range(2)]
        xrt = [sb(f"xrt{u}", [128, G, CW], BF16) for u in range(2)]
        if pos:
            xc = [sb(f"xc{u}", [P2, J, C], F32) for u in range(2)]
            sq = sb("sq", [P2, J, C], F32)
            xct = sb("xct", [128, W, H], BF16)
            st = [sb(f"st{u}", [P2, 4, J], F32) for u in range(2)]
            half = sb("half", [P2, J], F32)
        else:
            add = sb("add", [P2, NB4, J, C], F32)
        mirror = X[1][:, :, :, :].rearrange("p n j c -> p (n j c)")[:, 0:D * C].rearrange("p (m c) -> p m c", c=C)
        ident = sb("ident", [128, 128], F32)
        ident_b = sb("ident_b", [128, 128], BF16)
        cv_ps = [al.ps(f"cv_ps{u}", [128, 512], F32) for u in range(4)]
        tr_ps = [al.ps(f"tr_ps{u}", [128, 1024], BF16) for u in range(4)]

        zeroed, unit = sem("zeroed"), sem("unit")
        cleared = sem("cleared")
        strip_in, strip_out, taps_in = sem("strip_in"), sem("strip_out"), sem("taps_in")
        strip_one = sem("strip_one")
        band_zero, band_out = sem("band_zero"), sem("band_out")
        x_in = [sem(f"x_in{u}") for u in range(2)]
        add_in = sem("add_in")
        id_done = sem("id_done")
        conv_done = sem("conv_done")
        conv_out = sem("conv_out")
        tr_done = sem("tr_done")
        xr_sb, xc_sb = sem("xr_sb"), sem("xc_sb")
        mean_in, mean_sb, xc_done = sem("mean_in"), sem("mean_sb"), sem("xc_done")
        sq_done, var_in, var_sb, rs_done = sem("sq_done"), sem("var_in"), sem("var_sb"), sem("rs_done")
        xn_done, hi_done, lo_done = sem("xn_done"), sem("hi_done"), sem("lo_done")
        half_done = sem("half_done")
        x1_out = sem("x1_out")
        xr_out = [sem(f"xr_out{u}") for u in range(2)]
        xc_out = sem("xc_out")

        def tokens(dram, b):
            return dram[b].rearrange("(j r) w c -> (r w) j c", r=2)

        images = [(b, q) for b in range(NBATCH) for q in range(NB4)]
        block = ctx.enter_context(nc.Block())

        @block.sync
        def _(sp):
            def load(b):
                u = b % 2
                if b >= 2:
                    sp.wait_ge(lo_done, NB4 * (b - 1))
                    sp.wait_ge(hi_done, NB4 * (b - 1))
                    if pos:
                        sp.wait_ge(x1_out, 16 * NB4 * (b - 1))
                for q in range(NB4):
                    sp.dma_start(X[u][0:P2, q, 1:J + 1, :], tokens(src_d, NB4 * b + q)).then_inc(x_in[u], 16)

            def load_add(b):
                if b:
                    sp.wait_ge(conv_out, 16 * b)
                for q in range(NB4):
                    sp.dma_start(add[:, q], tokens(add_d, NB4 * b + q)).then_inc(add_in, 16)

            LAG = 2

            def store_t(n):
                sp.wait_ge(xr_sb, G * (n + 1))
                sp.dma_start(xr_d[G * n:G * n + G].rearrange("g p t -> p g t"), xrt[n % 2][:, :, :]).then_inc(
                    xr_out[n % 2], 16)
                if pos:
                    sp.wait_ge(xc_sb, G * (n + 1))
                    sp.dma_start(xc_d[G * n:G * n + G].rearrange("g p t -> p g t"),
                                 xct[:, :, :].rearrange("p (g l) h -> p g (l h)", g=G)).then_inc(xc_out, 16)

            sp.wait_ge(cleared, 1)
            zeros = T[:, :, :, :].rearrange("p d w c -> p (d w c)")[:, 0:D * W * BAND * C // 128]
            sp.dma_start(band_d.rearrange("d w v c -> (d w v c)").rearrange("(p n) -> p n", p=128),
                         zeros).then_inc(band_zero, 16)
            order = [0] + [d for d in range(-R, R + 1) if d]
            for n, dy in enumerate(order):
                for m in range(D):
                    sp.dma_start(mirror[n:n + 1, m, :], taps_d[dy + R, 2 * R - m]).then_inc(strip_in, 16)
            sp.wait_ge(strip_one, 1)
            sp.dma_start(mirror_d, mirror[0:D, :, :]).then_inc(strip_out, 16)
            sp.wait_ge(strip_out, 16)
            sp.wait_ge(band_zero, 16)
            for n in range(D):
                band, taps = band_d[n], mirror_d[n]
                sp.dma_start(bass.AP(band.tensor, band.offset, [[(BAND + 1) * C, W], [1, D * C]]),
                             bass.AP(taps.tensor, taps.offset, [[0, W], [1, D * C]])).then_inc(band_out, 16)
            sp.wait_ge(band_out, 16 * D)
            for d in range(3):
                for r in range(2):
                    for r2 in range(2):
                        dy = 2 * (d - 1) + r - r2
                        if abs(dy) > R:
                            continue
                        sp.dma_start(T[W * r:W * r + W, d, W * r2:W * r2 + W, :],
                                     band_d[order.index(dy), :, R:R + W, :]).then_inc(taps_in, 16)
            src = bass.AP(bias_d.tensor, bias_d.offset, [[C, 1], [0, P2], [1, C]])
            sp.dma_start(T[P2:P2 + 1, 1, :, :], src).then_inc(taps_in, 16)
            sp.wait_ge(cleared, 3)
            load(0)
            if not pos:
                load_add(0)
            sp.wait_ge(cleared, 5)
            load(1)
            for n, (b, q) in enumerate(images):
                if q == 0 and not pos and b + 1 < NBATCH:
                    load_add(b + 1)
                if q == 0 and b >= 1 and b + 1 < NBATCH:
                    load(b + 1)
                if pos:
                    sp.wait_ge(conv_out, 16 * (b + 1))
                    sp.dma_start(tokens(x1_d, n), X[b % 2][0:P2, q, 1:J + 1, :]).then_inc(x1_out, 16)
                if n >= LAG:
                    store_t(n - LAG)
            for n in range(B - LAG, B):
                store_t(n)
            for u in range(2):
                sp.wait_ge(xr_out[u], 16 * B // 2)
            if pos:
                sp.wait_ge(xc_out, 16 * B)
                sp.wait_ge(x1_out, 16 * B)

        NTAP = 1 + sum(abs(2 * (d - 1) + r - r2) <= R for d in range(3) for r in range(2) for r2 in range(2))

        @block.gpsimd
        def _(pool):
            identity_on(pool, ident, zeroed, unit)
            if pos:
                pool.memset(half[:, :], -0.5).then_inc(half_done, 1)
                pool.wait_ge(half_done, 1)
            for n, (b, q) in enumerate(images):
                u = n % 2
                if pos:
                    def lo(n):
                        u = n % 2
                        pool.wait_ge(hi_done, n + 1)
                        if n >= 2:
                            pool.wait_ge(tr_done, G * (n - 1))
                        pool.tensor_tensor(hl[u][:, :, C:2 * C], xc[u][:, :, :], hl[u][:, :, 0:C],
                                           ALU.subtract).then_inc(lo_done, 1)
                    pool.wait_ge(var_sb, n + 1)
                    pool.tensor_tensor(st[u][:, 3, :], st[u][:, 2, :], half[:, :], ALU.pow).then_inc(rs_done, 1)
                    if n:
                        lo(n - 1)
                    if n == B - 1:
                        lo(n)
                else:
                    pool.wait_ge(hi_done, n + 1)
                    if n >= 2:
                        pool.wait_ge(tr_done, G * (n - 1))
                    pool.tensor_tensor(hl[u][:, :, C:2 * C], X[b % 2][0:P2, q, 1:J + 1, :], hl[u][:, :, 0:C],
                                       ALU.subtract).then_inc(lo_done, 1)

        @block.tensor
        def _(pe):
            def conv(b, cg):
                u, t = b % 2, 16 * b + cg
                if cg == 0:
                    pe.wait_ge(x_in[u], 16 * NB4 * (b // 2 + 1))
                if t >= 4:
                    pe.wait_ge(conv_out, t - 3)
                for k in range(4):
                    c = 4 * cg + k
                    for d in (1, 0, 2):
                        kp = P2 + 1 if d == 1 else P2
                        ins = pe.matmul(cv_ps[t % 4][0:P2, P2 * k:P2 * k + P2].rearrange("p (n j) -> p n j", j=J),
                                        T[0:kp, d, :, c], X[u][0:kp, :, d:d + J, c], start=d == 1, stop=d == 2)
                ins.then_inc(conv_done, 1)

            pe.wait_ge(cleared, 3)
            pe.wait_ge(id_done, 1)
            pe.wait_ge(taps_in, 16 * NTAP)
            for cg in range(16):
                conv(0, cg)
            for n, (b, q) in enumerate(images):
                if b + 1 < NBATCH:
                    for cg in range(4):
                        conv(b + 1, 4 * q + cg)
                pe.wait_ge(lo_done, n + 1)
                for g in range(G):
                    t = G * n + g
                    if t >= 4:
                        pe.wait_ge(xr_sb, t - 3)
                        if pos:
                            pe.wait_ge(xc_sb, t - 3)
                    for j in range(PAIRS):
                        ins = pe.transpose(tr_ps[t % 4][:, P2 * j:P2 * j + P2], hl[n % 2][:, PAIRS * g + j, :],
                                           ident_b[0:P2, 0:P2])
                    ins.then_inc(tr_done, 1)

        @block.scalar
        def _(act):
            def conv_copy(b, cg):
                t = 16 * b + cg
                act.wait_ge(conv_done, t + 1)
                act.activation(X[b % 2][0:P2, :, 1:J + 1, 4 * cg:4 * cg + 4].rearrange("p n j c -> p c n j"),
                               cv_ps[t % 4][0:P2, 0:4 * P2].rearrange("p (c n j) -> p c n j", c=4, j=J),
                               ACT.Copy).then_inc(conv_out, 1)

            def high(n):
                b, q = images[n]
                if pos:
                    act.wait_ge(xn_done, n + 1)
                else:
                    act.wait_ge(conv_out, 16 * (b + 1))
                if n >= 2:
                    act.wait_ge(tr_done, G * (n - 1))
                src = xc[n % 2][:, :, :] if pos else X[b % 2][0:P2, q, 1:J + 1, :]
                act.activation(hl[n % 2][:, :, 0:C], src, ACT.Copy).then_inc(hi_done, 1)

            def row_copy(n):
                if n >= 2:
                    act.wait_ge(xr_out[n % 2], 16 * (n // 2))
                for g in range(G):
                    act.wait_ge(tr_done, G * n + g + 1)
                    act.activation(xrt[n % 2][:, g, :], tr_ps[(G * n + g) % 4][:, 0:CW],
                                   ACT.Copy).then_inc(xr_sb, 1)

            if pos:
                for cg in range(16):
                    conv_copy(0, cg)
            for n, (b, q) in enumerate(images):
                if pos:
                    act.wait_ge(xc_done, n + 1)
                    if n:
                        act.wait_ge(var_in, n)
                    act.activation(sq[:, :, :], xc[n % 2][:, :, :], ACT.Square).then_inc(sq_done, 1)
                    if n:
                        high(n - 1)
                        row_copy(n - 1)
                    if b + 1 < NBATCH:
                        for cg in range(4):
                            conv_copy(b + 1, 4 * q + cg)
                else:
                    high(n)
                    if n:
                        row_copy(n - 1)
            if pos:
                high(B - 1)
            row_copy(B - 1)

        @block.vector
        def _(dve):
            def conv_add(b, cg):
                t = 16 * b + cg
                if cg == 0:
                    dve.wait_ge(add_in, 16 * NB4 * (b + 1))
                dve.wait_ge(conv_done, t + 1)
                for k in range(4):
                    ins = dve.tensor_tensor(
                        X[b % 2][0:P2, :, 1:J + 1, 4 * cg + k],
                        cv_ps[t % 4][0:P2, P2 * k:P2 * k + P2].rearrange("p (n j) -> p n j", j=J),
                        add[:, :, :, 4 * cg + k], ALU.add)
                ins.then_inc(conv_out, 1)

            def center(n):
                b, q = images[n]
                u, x1 = n % 2, X[b % 2][0:P2, q, 1:J + 1, :]
                dve.wait_ge(conv_out, 16 * (b + 1))
                if n >= 2:
                    dve.wait_ge(rs_done, n - 1)
                dve.tensor_reduce(st[u][:, 0, :], x1, AX.X, ALU.add).then_inc(mean_in, 1)
                dve.wait_ge(mean_in, n + 1)
                dve.tensor_scalar(st[u][:, 1, :], st[u][:, 0, :], -1.0 / C, None, ALU.mult).then_inc(mean_sb, 1)
                dve.wait_ge(mean_sb, n + 1)
                if n >= 2:
                    dve.wait_ge(lo_done, n - 1)
                    dve.wait_ge(hi_done, n - 1)
                dve.tensor_tensor(xc[u][:, :, :], x1, st[u][:, 1, :].unsqueeze(2).to_broadcast([P2, J, C]),
                                  ALU.add).then_inc(xc_done, 1)

            def variance(n):
                u = n % 2
                dve.wait_ge(sq_done, n + 1)
                dve.tensor_reduce(st[u][:, 0, :], sq[:, :, :], AX.X, ALU.add).then_inc(var_in, 1)
                dve.wait_ge(var_in, n + 1)
                dve.tensor_scalar(st[u][:, 2, :], st[u][:, 0, :], 1.0 / C, EPS, ALU.mult, ALU.add).then_inc(var_sb, 1)

            def scale(n):
                u = n % 2
                dve.wait_ge(rs_done, n + 1)
                dve.tensor_tensor(xc[u][:, :, :], xc[u][:, :, :],
                                  st[u][:, 3, :].unsqueeze(2).to_broadcast([P2, J, C]), ALU.mult).then_inc(xn_done, 1)

            def col_copy(n):
                for g in range(G):
                    dve.wait_ge(tr_done, G * n + g + 1)
                    dve.wait_ge(xr_sb, G * n + g + 1)
                    if g == 0 and n:
                        dve.wait_ge(xc_out, 16 * n)
                    dve.tensor_copy(xct[:, :, LINES * g:LINES * g + LINES].rearrange("p w h -> p h w"),
                                    tr_ps[(G * n + g) % 4][:, 0:CW].rearrange("p (h w) -> p h w", w=W)).then_inc(xc_sb, 1)

            taps = T[:, :, :, :].rearrange("p d w c -> p (d w c)")
            dve.memset(X[1][:, :, :, :].rearrange("p n j c -> p (n j c)"), 0.0)
            dve.memset(taps, 0.0).then_inc(cleared, 1)
            dve.memset(X[0][96:128].rearrange("p n j c -> p (n j c)"), 1.0).then_inc(cleared, 1)
            dve.wait_ge(cleared, 2)
            dve.memset(X[0][:, :, 0:J + 2:J + 1, :], 0.0).then_inc(cleared, 1)
            dve.wait_ge(strip_in, 16 * D * D)
            if pos:
                mid = mirror[0:1, R, :]
                dve.tensor_scalar(mid, mid, 1.0, None, ALU.add).then_inc(strip_one, 1)
            else:
                dve.sem_inc(strip_one, 1)
            dve.wait_ge(unit, 1)
            dve.tensor_copy(ident_b[:, :], ident[:, :]).then_inc(id_done, 1)
            dve.wait_ge(strip_out, 16)
            dve.memset(X[1][96:128].rearrange("p n j c -> p (n j c)"), 1.0).then_inc(cleared, 1)
            dve.wait_ge(cleared, 4)
            dve.memset(X[1][:, :, 0:J + 2:J + 1, :], 0.0).then_inc(cleared, 1)
            if not pos:
                for cg in range(16):
                    conv_add(0, cg)
            for n, (b, q) in enumerate(images):
                if pos:
                    center(n)
                    if n:
                        scale(n - 1)
                    variance(n)
                    if n >= 2:
                        col_copy(n - 2)
                elif b + 1 < NBATCH:
                    for cg in range(4):
                        conv_add(b + 1, 4 * q + cg)
            if pos:
                scale(B - 1)
                col_copy(B - 2)
                col_copy(B - 1)


def mlp_phase(nc, tag, rt_d, x1_d, wo_d, bo_d, ln_g, ln_b, wf1_d, bf1_d, wf2_d, bf2_d, out_d):
    with ExitStack() as ctx:
        al = Alloc(nc, ctx, tag)
        sb, sem = al.sb, al.sem
        rt = [sb(f"rt{u}", [128, CW], BF16) for u in range(2)]
        x1 = [sb(f"x1{u}", [P2, PAIRS, C], F32) for u in range(2)]
        x2 = [sb(f"x2{u}", [P2, PAIRS, C], F32) for u in range(2)]
        x2b = [sb(f"x2b{u}", [P2, PAIRS, C], F32) for u in range(2)]
        xc = [sb(f"xc{u}", [P2, PAIRS, C], F32) for u in range(2)]
        sq = [sb(f"sq{u}", [P2, PAIRS, C], F32) for u in range(2)]
        st = [sb(f"st{u}", [P2, 5, PAIRS], F32) for u in range(2)]
        hl = [sb(f"hl{u}", [P2, PAIRS, 2 * C], BF16) for u in range(2)]
        yt = [sb(f"yt{u}", [128, CW], BF16) for u in range(2)]
        ht = [sb(f"ht{u}", [128, 2, CW], F32) for u in range(2)]
        o_sb = [sb(f"o{u}", [P2, PAIRS, C], F32) for u in range(2)]
        half = sb("half", [P2, PAIRS], F32)
        ident = sb("ident", [128, 128], F32)
        ident_b = sb("ident_b", [128, 128], BF16)
        wo_f = sb("wo_f", [128, C], F32)
        wo1 = sb("wo1", [128, C], BF16)
        wo2 = sb("wo2", [128, C], BF16)
        w1_f = sb("w1_f", [128, FF], F32)
        w1_g = sb("w1_g", [128, FF], F32)
        w11 = sb("w11", [128, FF], BF16)
        w12 = sb("w12", [128, FF], BF16)
        w2_p = sb("w2_p", [128, 2, 128], F32)
        g_c = sb("g_c", [128, 1], F32)
        b_c = sb("b_c", [128, 1], F32)
        b1_in = sb("b1_in", [128, 2], F32)
        b1 = sb("b1", [128, 2], F32)
        bo = sb("bo", [P2, C], F32)
        b2 = sb("b2", [P2, C], F32)

        o_ps = [al.ps(f"o_ps{u}", [128, 512], F32) for u in range(2)]
        t_ps = [al.ps(f"t_ps{u}", [128, 1024], BF16) for u in range(2)]
        h_ps = [al.ps(f"h_ps{u}", [128, 512], F32) for u in range(2)]
        y_ps = [al.ps(f"y_ps{u}", [128, 512], F32) for u in range(2)]

        par, zeroed, unit, prep, pre_pe, ready, half_done = (
            sem(n) for n in ("par", "zeroed", "unit", "prep", "pre_pe", "ready", "half_done"))
        rt_in = [sem(f"rt_in{u}") for u in range(2)]
        x1_in = [sem(f"x1_in{u}") for u in range(2)]
        out_st = [sem(f"out_st{u}") for u in range(2)]
        x1b_done, rs_done, lo_done, x2b_done = (sem(n) for n in ("x1b_done", "rs_done", "lo_done", "x2b_done"))
        o_done, t_done, fc1_done, fc2_done = (sem(n) for n in ("o_done", "t_done", "fc1_done", "fc2_done"))
        sq_done, hi_done, yt_done, gelu_done = (sem(n) for n in ("sq_done", "hi_done", "yt_done", "gelu_done"))
        x2_done, mean_in, mean_sb, xc_done = (sem(n) for n in ("x2_done", "mean_in", "mean_sb", "xc_done"))
        var_in, var_sb, xn_done, out_sb = (sem(n) for n in ("var_in", "var_sb", "xn_done", "out_sb"))

        passed = {mybir.EngineType.Pool: sem("passed_pool"), mybir.EngineType.SP: sem("passed_sp")}

        def cnt(i, v, per, plus):
            return i * (2 * per) + (v * per + plus)

        def nxt(i, v):
            return (i + 1, 0) if v else (i, 1)

        def prv(i, v):
            return (i, 0) if v else (i - 1, 1)

        def wait(eng, s, val):
            if not isinstance(val, int):
                eng.wait_ge(s, val)
                if eng.engine in passed:
                    eng.sem_inc(passed[eng.engine], 1)
            elif val > 0:
                eng.wait_ge(s, val)

        NI = NCH // 2

        def loop(eng, body):
            for v in range(2):
                body(0, v, v > 0, True)
            with eng.Fori(1, NI - 1) as i:
                for v in range(2):
                    body(i, v, True, True)
            for v in range(2):
                body(NI - 1, v, True, v < 1)

        x1_v = x1_d.rearrange("b (g j r) w c -> (b g) (r w) j c", g=G, r=2)
        out_v = out_d.rearrange("b (g j r) w c -> (b g) (r w) j c", g=G, r=2)
        block = ctx.enter_context(nc.Block())

        @block.sync
        def _(sp):
            def load(i, v):
                wait(sp, o_done, cnt(i, v, 1, -1))
                sp.dma_start(rt[v][:, :], rt_d[2 * i + v]).then_inc(rt_in[v], 16)
                wait(sp, x2_done, cnt(i, v, 1, -1))
                sp.dma_start(x1[v][:, :, :], x1_v[2 * i + v]).then_inc(x1_in[v], 16)

            def store(i, v):
                wait(sp, out_sb, cnt(i, v, 2, 2))
                sp.dma_start(out_v[2 * i + v], o_sb[v][:, :, :]).then_inc(out_st[v], 16)

            for h in range(2):
                p = slice(64 * h, 64 * h + 64)
                sp.dma_start(wo_f[p, :], wo_d).then_inc(par, 16)
                sp.dma_start(w1_f[p, :], wf1_d).then_inc(par, 16)
                sp.dma_start(g_c[p, :], ln_g.unsqueeze(1)).then_inc(par, 16)
                sp.dma_start(b_c[p, :], ln_b.unsqueeze(1)).then_inc(par, 16)
                sp.dma_start(w2_p[:, h, 0:C], wf2_d[128 * h:128 * h + 128, :]).then_inc(par, 16)
                sp.dma_start(b1_in[:, h:h + 1], bf1_d[128 * h:128 * h + 128].unsqueeze(1)).then_inc(par, 16)
            sp.dma_start(bo[:, :], bo_d.partition_broadcast(P2)).then_inc(par, 16)
            sp.dma_start(b2[:, :], bf2_d.partition_broadcast(P2)).then_inc(par, 16)
            load(0, 0)
            load(0, 1)

            def body(i, v, before, after):
                if not (isinstance(i, int) and i == NI - 1):
                    load(i + 1, v)
                if before:
                    store(*prv(i, v))

            loop(sp, body)
            store(NI - 1, 1)
            for v in range(2):
                sp.wait_ge(out_st[v], 16 * NI)

        @block.gpsimd
        def _(pool):
            def bias_o(i, v):
                wait(pool, x1_in[v], i * 16 + 16)
                pool.tensor_tensor(x1[v][:, :, :], x1[v][:, :, :], bo[:, :].unsqueeze(1).to_broadcast([P2, PAIRS, C]),
                                   ALU.add).then_inc(x1b_done, 1)

            def front(i, v):
                wait(pool, var_sb, cnt(i, v, 1, 1))
                pool.tensor_tensor(st[v][:, 4, :], st[v][:, 3, :], half[:, :], ALU.pow).then_inc(rs_done, 1)
                wait(pool, out_sb, cnt(i, v, 2, -2))
                pool.tensor_tensor(x2b[v][:, :, :], x2[v][:, :, :], b2[:, :].unsqueeze(1).to_broadcast([P2, PAIRS, C]),
                                   ALU.add).then_inc(x2b_done, 1)
                wait(pool, hi_done, cnt(i, v, 1, 1))
                pool.tensor_tensor(hl[v][:, :, C:2 * C], xc[v][:, :, :], hl[v][:, :, 0:C],
                                   ALU.subtract).then_inc(lo_done, 1)

            identity_on(pool, ident, zeroed, unit)
            pool.memset(half[:, :], -0.5).then_inc(half_done, 1)
            pool.wait_ge(half_done, 1)
            pool.wait_ge(par, 16 * 14)
            bias_o(0, 0)
            bias_o(0, 1)
            front(0, 0)

            def body(i, v, before, after):
                if after:
                    front(*nxt(i, v))
                if not (isinstance(i, int) and i == NI - 1):
                    bias_o(i + 1, v)

            loop(pool, body)

        @block.tensor
        def _(pe):
            def project(i, v):
                pe.wait_ge(rt_in[v], i * 16 + 16)
                wait(pe, x2_done, cnt(i, v, 1, -1))
                for j in range(PAIRS):
                    for n, w in enumerate((wo1, wo2)):
                        ins = pe.matmul(o_ps[v][0:P2, C * j:C * j + C], rt[v][:, P2 * j:P2 * j + P2], w[:, :],
                                        start=n == 0, stop=n == 1)
                ins.then_inc(o_done, 1)

            def turn(i, v):
                pe.wait_ge(lo_done, cnt(i, v, 1, 1))
                wait(pe, yt_done, cnt(i, v, 1, -1))
                for j in range(PAIRS):
                    ins = pe.transpose(t_ps[v][:, P2 * j:P2 * j + P2], hl[v][:, j, :], ident_b[0:P2, 0:P2])
                ins.then_inc(t_done, 1)

            def fc1(i, v):
                pe.wait_ge(yt_done, cnt(i, v, 1, 1))
                for h in range(2):
                    for f in range(2):
                        wait(pe, gelu_done, cnt(i, v, 4, 2 * h + f - 1))
                        cols = slice(HALF * h, HALF * h + HALF)
                        pe.matmul(h_ps[f][:, 0:HALF], w11[:, 128 * f:128 * f + 128], yt[v][:, cols],
                                  start=True, stop=False)
                        pe.matmul(h_ps[f][:, 0:HALF], w12[:, 128 * f:128 * f + 128], yt[v][:, cols],
                                  start=False, stop=True).then_inc(fc1_done, 1)

            def fc2(i, v):
                pe.wait_ge(gelu_done, cnt(i, v, 4, 4))
                for j in range(PAIRS):
                    if j % 4 == 0:
                        wait(pe, out_sb, cnt(i, v, 2, j // 4 - 1))
                    for f in range(2):
                        ins = pe.matmul(y_ps[j // 4][0:P2, 128 * (j % 4):128 * (j % 4) + 128],
                                        ht[v][:, f, P2 * j:P2 * j + P2], w2_p[:, f, :], start=f == 0, stop=f == 1)
                    if j in (3, 6):
                        ins.then_inc(fc2_done, 1)

            pe.wait_ge(par, 16 * 14)
            for f in range(2):
                ins = pe.matmul(h_ps[0][:, f:f + 1], w1_f[0:C, 128 * f:128 * f + 128], b_c[0:C, :],
                                start=True, stop=True)
            ins.then_inc(pre_pe, 1)
            pe.wait_ge(ready, 1)
            project(0, 0)

            def body(i, v, before, after):
                turn(i, v)
                if after:
                    project(*nxt(i, v))
                if before:
                    fc2(*prv(i, v))
                fc1(i, v)

            loop(pe, body)
            fc2(NI - 1, 1)

        @block.scalar
        def _(act):
            def square(i, v):
                act.wait_ge(xc_done, cnt(i, v, 1, 1))
                wait(act, var_in, cnt(i, v, 1, -1))
                act.activation(sq[v][:, :, :], xc[v][:, :, :], ACT.Square).then_inc(sq_done, 1)

            def high(i, v):
                act.wait_ge(xn_done, cnt(i, v, 1, 1))
                wait(act, t_done, cnt(i, v, 1, -1))
                act.activation(hl[v][:, :, 0:C], xc[v][:, :, :], ACT.Copy).then_inc(hi_done, 1)

            act.wait_ge(ready, 1)
            square(0, 0)
            high(0, 0)

            def body(i, v, before, after):
                act.wait_ge(t_done, cnt(i, v, 1, 1))
                wait(act, fc1_done, cnt(i, v, 4, -4))
                act.activation(yt[v][:, :], t_ps[v][:, 0:CW], ACT.Copy).then_inc(yt_done, 1)
                if after:
                    square(*nxt(i, v))
                for h in range(2):
                    for f in range(2):
                        act.wait_ge(fc1_done, cnt(i, v, 4, 2 * h + f + 1))
                        wait(act, fc2_done, cnt(i, v, 2, -2))
                        act.activation(ht[v][:, f, HALF * h:HALF * h + HALF], h_ps[f][:, 0:HALF], ACT.Gelu,
                                       bias=b1[:, f:f + 1]).then_inc(gelu_done, 1)
                    if h == 0 and after:
                        high(*nxt(i, v))

            loop(act, body)

        @block.vector
        def _(dve):
            def front(i, v):
                dve.wait_ge(o_done, cnt(i, v, 1, 1))
                dve.wait_ge(x1b_done, cnt(i, v, 1, 1))
                wait(dve, x2b_done, cnt(i, v, 1, -1))
                dve.tensor_tensor(x2[v][:, :, :], o_ps[v][0:P2, 0:PAIRS * C].rearrange("p (j c) -> p j c", c=C),
                                  x1[v][:, :, :], ALU.add).then_inc(x2_done, 1)
                dve.wait_ge(x2_done, cnt(i, v, 1, 1))
                dve.tensor_reduce(st[v][:, 0, :], x2[v][:, :, :], AX.X, ALU.add).then_inc(mean_in, 1)
                dve.wait_ge(mean_in, cnt(i, v, 1, 1))
                dve.tensor_scalar(st[v][:, 1, :], st[v][:, 0, :], -1.0 / C, None, ALU.mult).then_inc(mean_sb, 1)
                dve.wait_ge(mean_sb, cnt(i, v, 1, 1))
                wait(dve, lo_done, cnt(i, v, 1, -1))
                dve.tensor_tensor(xc[v][:, :, :], x2[v][:, :, :],
                                  st[v][:, 1, :].unsqueeze(2).to_broadcast([P2, PAIRS, C]), ALU.add).then_inc(xc_done, 1)

            def variance(i, v):
                dve.wait_ge(sq_done, cnt(i, v, 1, 1))
                dve.tensor_reduce(st[v][:, 2, :], sq[v][:, :, :], AX.X, ALU.add).then_inc(var_in, 1)
                dve.wait_ge(var_in, cnt(i, v, 1, 1))
                wait(dve, rs_done, cnt(i, v, 1, -1))
                dve.tensor_scalar(st[v][:, 3, :], st[v][:, 2, :], 1.0 / C, EPS, ALU.mult, ALU.add).then_inc(var_sb, 1)

            def scale(i, v):
                dve.wait_ge(rs_done, cnt(i, v, 1, 1))
                dve.tensor_tensor(xc[v][:, :, :], xc[v][:, :, :],
                                  st[v][:, 4, :].unsqueeze(2).to_broadcast([P2, PAIRS, C]), ALU.mult).then_inc(xn_done, 1)

            def result(i, v):
                dve.wait_ge(x2b_done, cnt(i, v, 1, 1))
                wait(dve, out_st[v], i * 16)
                for n, (a, b) in enumerate(((0, 4), (4, 7))):
                    dve.wait_ge(fc2_done, cnt(i, v, 2, n + 1))
                    dve.tensor_tensor(
                        o_sb[v][:, a:b, :],
                        y_ps[n][0:P2, 0:128 * (b - a)].rearrange("p (j c) -> p j c", c=128)[:, :, 0:C],
                        x2b[v][:, a:b, :], ALU.add).then_inc(out_sb, 1)

            step = [0]

            def done(ins):
                step[0] += 1
                ins.then_inc(prep, 1)

            def settled():
                dve.wait_ge(prep, step[0])

            done(dve.memset(wo2[:, :], 0.0))
            done(dve.memset(w12[:, :], 0.0))
            done(dve.memset(w2_p[:, :, C:128], 0.0))
            dve.wait_ge(par, 16 * 14)
            done(dve.tensor_copy(wo1[:, :], wo_f[:, :]))
            done(dve.tensor_scalar(w1_g[:, :], w1_f[:, :], g_c[:, 0:1], None, ALU.mult))
            settled()
            done(dve.tensor_tensor(wo2[0:64, :], wo_f[0:64, :], wo1[0:64, :], ALU.subtract))
            done(dve.tensor_copy(w11[:, :], w1_g[:, :]))
            settled()
            done(dve.tensor_tensor(w12[0:64, :], w1_g[0:64, :], w11[0:64, :], ALU.subtract))
            dve.wait_ge(pre_pe, 1)
            done(dve.tensor_tensor(b1[:, :], h_ps[0][:, 0:2], b1_in[:, :], ALU.add))
            dve.wait_ge(unit, 1)
            done(dve.tensor_copy(ident_b[:, :], ident[:, :]))
            settled()
            dve.sem_inc(ready, 1)
            front(0, 0)
            variance(0, 0)
            scale(0, 0)

            def body(i, v, before, after):
                if after:
                    front(*nxt(i, v))
                    variance(*nxt(i, v))
                if before:
                    result(*prv(i, v))
                if after:
                    scale(*nxt(i, v))

            loop(dve, body)
            result(NI - 1, 1)


def build(nc, x, mask_h, mask_w, pos_w, pos_b, ln1_g, ln1_b, q_w, q_b, k_w, k_b, v_w, v_b, lepe_w, lepe_b,
          out_w, out_b, ln2_g, ln2_b, fc1_w, fc1_b, fc2_w, fc2_b, out):
    def scratch(name, shape, dt):
        return nc.dram_tensor(name, shape, dt).ap()

    x1_d = scratch("x1_scratch", [B, H, W, C], F32)
    v_d = scratch("v_scratch", [B, H, W, C], F32)
    row_d = scratch("row_attention", [B, H, W, C], F32)
    att_d = scratch("attention", [B, H, W, C], F32)
    xr_d = scratch("xn_rows", [NCH, 128, CW], BF16)
    xc_d = scratch("xn_cols", [NCH, 128, CW], BF16)
    rt_d = scratch("r_rows", [NCH, 128, CW], BF16)
    mirror1_d, band1_d = scratch("pos_mirrored", [3, 3, C], F32), scratch("pos_band", [3, W, W + 2, C], F32)
    mirror2_d, band2_d = scratch("lepe_mirrored", [5, 5, C], F32), scratch("lepe_band", [5, W, W + 4, C], F32)
    qkv = [q_w, k_w, v_w], [q_b, k_b, v_b]
    conv_phase(nc, "pos", True, x, pos_w.rearrange("a b o c -> a b (o c)"), pos_b, None, mirror1_d, band1_d, x1_d, xr_d, xc_d)
    attention_phase(nc, "rows", True, xr_d, mask_w, *qkv, ln1_g, ln1_b, v_d, row_d)
    attention_phase(nc, "cols", False, xc_d, mask_h, *qkv, ln1_g, ln1_b, row_d, att_d)
    conv_phase(nc, "lepe", False, v_d, lepe_w.rearrange("a b o c -> a b (o c)"), lepe_b, att_d, mirror2_d, band2_d,
               None, rt_d, None)
    mlp_phase(nc, "mlp", rt_d, x1_d, out_w, out_b, ln2_g, ln2_b, fc1_w, fc1_b, fc2_w, fc2_b, out)


_INS = ["x"] + ["L0_conv_" + n for n in (
    "mask_h", "mask_w", "pos_w", "pos_b", "ln1_g", "ln1_b", "q_w", "q_b", "k_w", "k_b", "v_w", "v_b", "lepe_w",
    "lepe_b", "out_w", "out_b", "ln2_g", "ln2_b", "fc1_w", "fc1_b", "fc2_w", "fc2_b")]
_OUTS = [((B, H, W, C), "float32")]


def kernel(**inputs):
    import numpy as _np
    import concourse.bacc as _bacc
    from concourse import mybir as _mybir
    from concourse.bass_utils import run_bass_kernel_spmd as _run

    nc = _bacc.Bacc("TRN2", target_bir_lowering=False, num_devices=1)
    arrays, args = {}, []
    for name in _INS:
        a = _np.ascontiguousarray(inputs[name])
        arrays[f"in_{name}_dram"] = a
        args.append(nc.dram_tensor(f"in_{name}_dram", a.shape, _mybir.dt.from_np(a.dtype), kind="ExternalInput").ap())
    for i, (shape, dtype) in enumerate(_OUTS):
        dt = _mybir.dt.from_np(_np.dtype(dtype))
        args.append(nc.dram_tensor(f"out_{i}_dram", shape, dt, kind="ExternalOutput").ap())
    build(nc, *args)
    r = _run(nc, [arrays], core_ids=[0])
    got = tuple(r.results[0][f"out_{i}_dram"] for i in range(len(_OUTS)))
    return got[0]
```

```python
from contextlib import ExitStack

import concourse.bass as bass
from concourse import mybir

F32 = mybir.dt.float32
BF16 = mybir.dt.bfloat16
ALU = mybir.AluOpType
ACT = mybir.ActivationFunctionType
AX = mybir.AxisListType

B, H, W, C = 16, 56, 56, 64
NH, KD, FF = 8, 8, 256
EPS = 1e-6
SCALE = KD ** -0.5
L = 56
LINES = 14
PAIRS = LINES // 2
G = H // LINES
NCH = B * G
CW = LINES * L
HALF = CW // 2
S8 = NH * L
VW = 4 * 36
TAIL = 60


class Alloc:

    def __init__(self, nc, ctx, tag):
        self.nc, self.ctx, self.tag, self.sems = nc, ctx, tag, []
        ctx.callback(self.close)

    def close(self):
        self.nc.all_engine_barrier()
        self.nc.clear_and_free_semaphores(self.sems)
        self.nc.all_engine_barrier()

    def sb(self, name, shape, dt):
        return self.ctx.enter_context(self.nc.sbuf_tensor(f"{self.tag}_{name}", shape, dt))

    def ps(self, name, shape, dt):
        return self.ctx.enter_context(self.nc.psum_tensor(f"{self.tag}_{name}", shape, dt))

    def sem(self, name):
        self.sems.append(self.nc.alloc_semaphore(f"{self.tag}_{name}"))
        return self.sems[-1]


def identity_on(pool, ident, zeroed, made):
    pool.memset(ident[:, :], 0.0).then_inc(zeroed, 1)
    pool.wait_ge(zeroed, 1)
    pool.affine_select(out=ident[:, :], in_=ident[:, :], compare_op=ALU.not_equal, fill=1.0, base=0,
                       pattern=[[-1, 128]], channel_multiplier=1).then_inc(made, 1)


def attention_phase(nc, tag, rows, xt_d, mask_d, w_d, b_d, ln_g, ln_b, v_d, out_d):
    with ExitStack() as ctx:
        al = Alloc(nc, ctx, tag)
        sb, sem = al.sb, al.sem
        xt = [sb(f"xt{u}", [128, CW], BF16) for u in range(2)]
        k_hilo = [sb(f"k_hilo{v}", [128, CW], BF16) for v in range(4)]
        k_unit = [sb(f"k_unit{v}", [128, CW], BF16) for v in range(4)]
        q_unit = [sb(f"q_unit{u}", [128, CW], BF16) for u in range(2)]
        q_src = [sb(f"q_src{u}", [128, 2, CW], BF16) for u in range(2)]
        kx = [sb(f"kx{u}", [128, NH, CW], BF16) for u in range(2)]
        qx = [sb(f"qx{u}", [128, 2, NH, CW], BF16) for u in range(2)]
        vf = [sb(f"vf{u}", [128, PAIRS * C], F32) for u in range(2)]
        vx = [sb(f"vx{v}", [128, PAIRS * VW + TAIL], F32) for v in range(4)]
        mx = [sb(f"mx{u}", [128, 2, NH, L], BF16) for u in range(2)]
        mm = [sb(f"mm{u}", [128, 128], F32) for u in range(2)]
        prob = [sb(f"prob{t}", [128, NH, 64], F32) for t in range(4)]
        o_sb = [sb(f"o_sb{u}", [128, 2, PAIRS, 32], F32) for u in range(2)]
        rec = [sb(f"rec{u}", [128, 3 * 8], F32) for u in range(2)]
        ident = sb("ident", [128, 128], F32)
        pick = sb("pick", [128, PAIRS, L], BF16)
        negd = sb("negd", [128, NH], F32)
        sel7 = sb("sel7", [128, PAIRS], F32)
        mask_f = sb("mask_f", [128, NH, L], F32)
        mlo_hi = sb("mlo_hi", [128, NH, L], BF16)
        mlo = sb("mlo", [128, NH, L], BF16)
        wf = [sb(f"wf{n}", [128, C], F32) for n in "qkv"]
        wg = [sb(f"wg{n}", [128, C], F32) for n in "qkv"]
        w1 = [sb(f"w1{n}", [128, 2 * C], BF16) for n in "qkv"]
        w2 = [sb(f"w2{n}", [128, 2 * C], BF16) for n in "qkv"]
        wdup = [sb(f"wdup{n}", [C, 2 * C], F32) for n in "qk"]
        g_c = sb("g_c", [128, 1], F32)
        b_c = sb("b_c", [128, 1], F32)
        b_wide = sb("b_wide", [C, 128], F32)
        b_in = sb("b_in", [128, 2], F32)
        bias = sb("bias", [128, 2], F32)
        bv_in = sb("bv_in", [128, C], F32)
        bv = sb("bv", [128, C], F32)

        s_ps = [al.ps(f"s_ps{u}", [128, 512], F32) for u in range(2)]
        st_ps = [al.ps(f"st_ps{u}", [128, 512], F32) for u in range(2)]
        pv_ps = [al.ps(f"pv_ps{u}", [128, 512], F32) for u in range(2)]
        pj = [al.ps(f"pj{u}", [128, 512], F32) for u in range(2)]

        par, mask_in = sem("par"), sem("mask_in")
        zeroed, unit = sem("zeroed"), sem("unit")
        cleared = sem("cleared")
        x_clear = sem("x_clear")
        x_mask = sem("x_mask")
        weights = sem("weights")
        prep = sem("prep")
        pre_pe = sem("pre_pe")
        ones_set = sem("ones_set")
        eyes = sem("eyes")
        ready = sem("ready")
        xt_in = [sem(f"xt_in{u}") for u in range(2)]
        kx_in = [sem(f"kx_in{u}") for u in range(2)]
        qx_in = [sem(f"qx_in{u}") for u in range(2)]
        kx_in_sw = [sem(f"kx_in_sw{u}") for u in range(2)]
        qx_in_sw = [sem(f"qx_in_sw{u}") for u in range(2)]
        v_io = [sem(f"v_io{u}") for u in range(2)]
        o_out = [sem(f"o_out{u}") for u in range(2)]
        k_proj, q_proj, v_proj = sem("k_proj"), sem("q_proj"), sem("v_proj")
        s_done, mt_done = sem("s_done"), sem("mt_done")
        st_done, pv_done = sem("st_done"), sem("pv_done")
        k_hi, q_hi, exp_done = sem("k_hi"), sem("q_hi"), sem("exp_done")
        k_lo, k_cp = sem("k_lo"), sem("k_cp")
        q_lo, q_cp = sem("q_lo"), sem("q_cp")
        v_sb = sem("v_sb")
        max_done, mx_done = sem("max_done"), sem("mx_done")
        rec_done, norm_done = sem("rec_done"), sem("norm_done")
        vx_done = sem("vx_done")

        def lines(t):
            return (t if isinstance(t, bass.AP) else t[:, :]).rearrange("p (l q) -> p l q", q=L)

        def chunk_tokens(dram, i, v):
            if rows:
                return dram.rearrange("b (g l) q c -> (b g) q l c", l=LINES)[4 * i + v]
            return dram.rearrange("b q (g l) c -> b g q l c", l=LINES)[i, v]

        def loop(eng, body, first):
            first()
            for v in range(4):
                body(0, v, True, True)
            with eng.Fori(1, B - 1) as i:
                for v in range(4):
                    body(i, v, True, True)
            for v in range(4):
                body(B - 1, v, v < 3, v < 2)

        passed = {mybir.EngineType.Pool: sem("passed_pool"), mybir.EngineType.SP: sem("passed_sp")}

        def cnt(i, v, per, plus):
            return i * (4 * per) + (v * per + plus)

        def nxt(i, v, d):
            return (i + 1, v + d - 4) if v + d >= 4 else (i, v + d)

        def wait(eng, s, val):
            if not isinstance(val, int):
                eng.wait_ge(s, val)
                if eng.engine in passed:
                    eng.sem_inc(passed[eng.engine], 1)
            elif val > 0:
                eng.wait_ge(s, val)

        AHEAD = ((0, 1), (2,), (3,), (4,), (5, 6), (), ())
        MAXIMA_AT = 5

        block = ctx.enter_context(nc.Block())

        def fill_k(eng, i, v, slots, sems):
            u = v % 2
            wait(eng, k_cp, cnt(i, v, 1, 1))
            wait(eng, s_done, cnt(i, v, 7, -7))
            for s in slots:
                n = 4 * (s % 2) + s // 2
                eng.dma_start(kx[u][8 * n:8 * n + 8, s, :], k_hilo[v][8 * n:8 * n + 8, :]).then_inc(sems[u], 16)

        def fill_q(eng, i, v, slots, high, sems):
            u = v % 2
            wait(eng, q_cp, cnt(i, v, 1, 1))
            wait(eng, st_done, cnt(i, v, 7, -7))
            for s in slots:
                n = 4 * (s % 2) + s // 2
                eng.dma_start(qx[u][8 * n:8 * n + 8, :, s, :], q_src[u][8 * n:8 * n + 8, :, :]).then_inc(sems[u], 16)
            for s in high:
                n = 4 * (s % 2) + s // 2
                eng.dma_start(qx[u][64 + 8 * n:72 + 8 * n, 1, s, :],
                              q_src[u][64 + 8 * n:72 + 8 * n, 1, :]).then_inc(sems[u], 16)

        def filled(eng, s, s_sw, i, v, sp_n, pool_n):
            u = v % 2
            for x, n in ((s[u], 16 * sp_n), (s_sw[u], 16 * pool_n)):
                wait(eng, x, i * 2 * n + (v // 2 + 1) * n)

        K_SP, K_POOL = range(0, 5), range(5, 8)
        Q_SP, Q_POOL = (range(0, 5), range(0, 5)), (range(5, 8), range(5, 8))
        NK_SP, NK_POOL = len(K_SP), len(K_POOL)
        NQ_SP, NQ_POOL = sum(map(len, Q_SP)), sum(map(len, Q_POOL))

        @block.sync
        def _(sp):
            def load_x(i, v):
                u = v % 2
                if rows:
                    wait(sp, v_proj, cnt(i, v, 1, -1))
                else:
                    wait(sp, q_proj, cnt(i, v, 2, -2))
                sp.dma_start(xt[u][:, :], xt_d[4 * i + v]).then_inc(xt_in[u], 16)

            def load_v(i, v):
                u = v % 2
                wait(sp, vx_done, cnt(i, v, 4, -4))
                src = chunk_tokens(v_d, i, v)
                for r in range(2):
                    sp.dma_start(vf[u][64 * r:64 * r + L, :].rearrange("p (j c) -> p j c", c=C),
                                 src[:, PAIRS * r:PAIRS * r + PAIRS, :]).then_inc(v_io[u], 16)

            def store_v(i, v):
                u = v % 2
                wait(sp, v_sb, cnt(i, v, 1, 1))
                dst = chunk_tokens(v_d, i, v)
                for r in range(2):
                    sp.dma_start(dst[:, PAIRS * r:PAIRS * r + PAIRS, :],
                                 vf[u][64 * r:64 * r + L, :].rearrange("p (j c) -> p j c", c=C)).then_inc(v_io[u], 16)

            def store_o(i, v):
                u = v % 2
                wait(sp, norm_done, cnt(i, v, 6, 6))
                dst = chunk_tokens(out_d, i, v)
                for h in range(2):
                    sp.dma_start(dst[:, :, 32 * h:32 * h + 32],
                                 o_sb[u][64 * h:64 * h + L].rearrange("p r j c -> p (r j) c")).then_inc(o_out[u], 16)

            def first():
                for n in range(3):
                    for h in range(2):
                        sp.dma_start(wf[n][64 * h:64 * h + 64, :], w_d[n]).then_inc(par, 16)
                    if n < 2:
                        for h in range(2):
                            sp.dma_start(b_in[64 * h:64 * h + 64, n:n + 1], b_d[n].unsqueeze(1)).then_inc(par, 16)
                for h in range(2):
                    sp.dma_start(g_c[64 * h:64 * h + 64, :], ln_g.unsqueeze(1)).then_inc(par, 16)
                    sp.dma_start(b_c[64 * h:64 * h + 64, :], ln_b.unsqueeze(1)).then_inc(par, 16)
                sp.dma_start(bv_in[:, :], b_d[2].partition_broadcast(128)).then_inc(par, 16)
                load_x(0, 0)
                load_x(0, 1)
                m = mask_d.rearrange("(i a) q k -> q i a k", i=2)
                for h in range(2):
                    for i in range(2):
                        sp.dma_start(mask_f[64 * h:64 * h + L].rearrange("p (a i) k -> p i a k", i=2)[:, i],
                                     m[:, i]).then_inc(mask_in, 16)
                if not rows:
                    load_v(0, 0)
                    load_v(0, 1)
                sp.wait_ge(x_clear, 1)
                fill_k(sp, 0, 0, K_SP, kx_in)
                sp.wait_ge(x_clear, 2)
                fill_q(sp, 0, 0, *Q_SP, qx_in)
                sp.wait_ge(x_clear, 4)
                fill_k(sp, 0, 1, K_SP, kx_in)
                load_x(0, 2)
                if rows:
                    store_v(0, 0)
                    store_v(0, 1)

            def body(i, v, more_s, more_p):
                if more_p and not (isinstance(i, int) and i == B - 1 and v >= 1):
                    load_x(*nxt(i, v, 3))
                if more_s:
                    fill_q(sp, *nxt(i, v, 1), *Q_SP, qx_in)
                if not (isinstance(i, int) and i == 0 and v == 0):
                    store_o(*(nxt(i, v, -1) if v else (i - 1, 3)))
                if more_p:
                    if not rows:
                        load_v(*nxt(i, v, 2))
                    fill_k(sp, *nxt(i, v, 2), K_SP, kx_in)
                    if rows:
                        store_v(*nxt(i, v, 2))

            loop(sp, body, first)
            store_o(B - 1, 3)
            for u in range(2):
                sp.wait_ge(o_out[u], 32 * (NCH // 2))
                if rows:
                    sp.wait_ge(v_io[u], 32 * (NCH // 2))

        @block.gpsimd
        def _(pool):
            def build_vx(i, v):
                u = v % 2
                if rows:
                    wait(pool, v_sb, cnt(i, v, 1, 1))
                else:
                    wait(pool, v_io[u], i * 64 + (v // 2) * 32 + 32)
                wait(pool, pv_done, cnt(i, v, 7, -21))
                dst = vx[v][:, 0:PAIRS * VW].rearrange("p (j a i r d) -> p j a i r d", a=4, i=2, r=2, d=9)
                src = vf[u][:, :].rearrange("p (j i a d) -> p j a i d", i=2, a=4, d=8)
                for r in range(2):
                    rows_ = slice(64 * r, 64 * r + L)
                    for h in range(2):
                        pool.tensor_copy(dst[rows_, :, :, h, r, 0:8], src[rows_, :, :, h, :]).then_inc(vx_done, 1)

            def first():
                identity_on(pool, ident, zeroed, unit)
                for t, dims in ((kx[0], "p s t -> p (s t)"), (qx[0], "p n s t -> p (n s t)"),
                                (kx[1], "p s t -> p (s t)"), (qx[1], "p n s t -> p (n s t)")):
                    pool.memset(t[(slice(None),) * len(t.shape)].rearrange(dims).bitcast(F32), 0.0).then_inc(x_clear, 1)
                pool.wait_ge(x_clear, 4)
                fill_k(pool, 0, 0, K_POOL, kx_in_sw)
                fill_q(pool, 0, 0, *Q_POOL, qx_in_sw)
                pool.wait_ge(ones_set, 1)
                build_vx(0, 0)
                build_vx(0, 1)
                fill_k(pool, 0, 1, K_POOL, kx_in_sw)

            def body(i, v, more_s, more_p):
                if more_s:
                    fill_q(pool, *nxt(i, v, 1), *Q_POOL, qx_in_sw)
                if more_p:
                    fill_k(pool, *nxt(i, v, 2), K_POOL, kx_in_sw)
                    build_vx(*nxt(i, v, 2))

            loop(pool, body, first)

        @block.tensor
        def _(pe):
            def project(i, v, n, done, free):
                u = v % 2
                for h in range(2):
                    cols = slice(HALF * h, HALF * h + HALF)
                    for s, val in free(h):
                        wait(pe, s, val)
                    pe.matmul(pj[h][:, 0:HALF], w1[n][:, :], xt[u][:, cols], start=True, stop=False)
                    pe.matmul(pj[h][:, 0:HALF], w2[n][:, :], xt[u][:, cols], start=False, stop=True).then_inc(done, 1)

            def project_k(i, v):
                pe.wait_ge(xt_in[v % 2], i * 32 + (v // 2) * 16 + 16)
                if rows:
                    project(i, v, 1, k_proj, lambda h: [(v_sb, cnt(i, v, 1, 0))] if h == 0 else
                            [(q_lo, cnt(i, v, 2, 0))])
                else:
                    project(i, v, 1, k_proj, lambda h: [(q_lo, cnt(i, v, 2, h - 1))])

            def project_q(i, v):
                project(i, v, 0, q_proj, lambda h: [(k_lo, cnt(i, v, 2, h + 1))])

            def project_v(i, v):
                wait(pe, q_lo, cnt(i, v, 2, 1))
                x = lines(xt[v % 2])
                for j in range(PAIRS):
                    for part, w in enumerate((w1[2], w2[2])):
                        for r in range(2):
                            ins = pe.matmul(pj[0][64 * r:64 * r + L, C * j:C * j + C], x[:, PAIRS * r + j, :],
                                            w[:, 0:C], start=part == 0, stop=part == 1)
                ins.then_inc(v_proj, 1)

            def scores(i, v, j):
                u = v % 2
                if j == 0:
                    filled(pe, kx_in, kx_in_sw, i, v, NK_SP, NK_POOL)
                    wait(pe, q_cp, cnt(i, v, 1, 1))
                if j == 1:
                    wait(pe, mx_done, cnt(i, v, 2, 0))
                else:
                    wait(pe, max_done, cnt(i, v, 7, j - 1 if j else 0))
                q, k = lines(q_unit[u]), kx[u][:, :, :].rearrange("p s (l q) -> p s l q", q=L)
                for r in range(2):
                    ins = pe.matmul(s_ps[j % 2][64 * r:64 * r + L, 0:S8].rearrange("p (s k) -> p s k", k=L),
                                    q[0:120, PAIRS * r + j, :], k[0:120, :, PAIRS * r + j, :],
                                    start=True, stop=True)
                ins.then_inc(s_done, 1)

            def maxima(i, v):
                pe.wait_ge(max_done, cnt(i, v, 7, 7))
                pe.transpose(s_ps[1][0:120, 0:128], mm[v % 2][:, 0:120], ident[:, :]).then_inc(mt_done, 1)

            def scores_t(i, v, j):
                u, t = v % 2, 7 * v + j
                if j == 0:
                    filled(pe, qx_in, qx_in_sw, i, v, NQ_SP, NQ_POOL)
                    pe.wait_ge(mx_done, cnt(i, v, 2, 2))
                wait(pe, exp_done, i * 28 + t - 1)
                kh, ku = lines(k_hilo[v]), lines(k_unit[v])
                q = qx[u][:, :, :, :].rearrange("p t s (l q) -> p t s l q", q=L)
                out = st_ps[t % 2][:, 0:S8].rearrange("p (s q) -> p s q", q=L)
                for n in range(3):
                    for r in range(2):
                        ln = PAIRS * r + j
                        lhs, rhs = ((kh[:, ln, :], q[:, 1, :, ln, :]),
                                    (ku[0:120, ln, :], q[0:120, 0, :, ln, :]),
                                    (pick[0:120, j, :], mx[u][0:120, r, :, :]))[n]
                        ins = pe.matmul(out[64 * r:64 * r + L], lhs, rhs, start=n == 0, stop=n == 2)
                ins.then_inc(st_done, 1)

            def products(i, v, j):
                t, g = 7 * v + j, 3 * v + j // 3
                if j == 0:
                    pe.wait_ge(vx_done, cnt(i, v, 4, 4))
                if j % 3 == 0:
                    wait(pe, norm_done, i * 24 + 2 * g - 2)
                pe.wait_ge(exp_done, i * 28 + t + 1)
                for a in range(4):
                    at = VW * (j % 3) + 36 * a
                    ins = pe.matmul(pv_ps[g % 2][0:120, at:at + 96],
                                    prob[t % 4][:, 2 * a:2 * a + 2, :].rearrange("p i q -> p (i q)")[:, 0:120],
                                    vx[v][:, VW * j + 36 * a:VW * j + 36 * a + 96], start=True, stop=True)
                ins.then_inc(pv_done, 1)

            def first():
                pe.wait_ge(cleared, 1)
                pe.wait_ge(par, 16 * 15)
                pe.wait_ge(prep, 2)
                for n in range(2):
                    pe.matmul(s_ps[1][:, n:n + 1], wdup[n][:, :], b_c[0:C, :], start=True, stop=True)
                pe.matmul(s_ps[1][:, C:2 * C], b_wide[:, :], wf[2][0:C, :], start=True, stop=True).then_inc(pre_pe, 1)
                pe.wait_ge(weights, 1)
                project_k(0, 0)
                pe.wait_ge(mask_in, 16 * 4)
                pe.wait_ge(unit, 1)
                for h in range(2):
                    for s in range(NH):
                        ins = pe.matmul(s_ps[0][64 * h:64 * h + L, L * s:L * s + L], mask_f[0:L, s, :],
                                        ident[0:L, 0:L], start=True, stop=True)
                ins.then_inc(pre_pe, 1)
                for v in range(2):
                    if v:
                        project_k(0, v)
                    project_q(0, v)
                    if rows:
                        project_v(0, v)
                pe.wait_ge(ready, 1)
                pe.wait_ge(x_mask, NH)
                pe.wait_ge(eyes, 6)
                for j in range(PAIRS):
                    scores(0, 0, j)
                maxima(0, 0)
                pe.wait_ge(x_mask, 2 * NH)
                pe.wait_ge(ready, 2)

            def body(i, v, more_s, more_p):
                n1, n2 = nxt(i, v, 1), nxt(i, v, 2)
                for j in range(PAIRS):
                    scores_t(i, v, j)
                    if j:
                        products(i, v, j - 1)
                    elif not (isinstance(i, int) and i == 0 and v == 0):
                        products(*nxt(i, v, -1) if v else (i - 1, 3), PAIRS - 1)
                    if more_p and j == 0:
                        project_k(*n2)
                    if more_s:
                        for m in AHEAD[j]:
                            scores(*n1, m)
                        if j == MAXIMA_AT:
                            maxima(*n1)
                    if more_p and j == 1:
                        project_q(*n2)
                    if rows and more_p and j == 3:
                        project_v(*n2)

            loop(pe, body, first)
            products(B - 1, 3, PAIRS - 1)

        @block.scalar
        def _(act):
            def high_k(i, v):
                wait(act, s_done, cnt(i, v, 7, -21))
                wait(act, st_done, cnt(i, v, 7, -21))
                for h in range(2):
                    cols = slice(HALF * h, HALF * h + HALF)
                    act.wait_ge(k_proj, cnt(i, v, 2, h + 1))
                    act.activation(k_hilo[v][:, cols], pj[h][:, 0:HALF], ACT.Identity,
                                   bias=bias[:, 1:2]).then_inc(k_hi, 1)

            def high_q(i, v):
                u = v % 2
                if isinstance(i, int) and i == 0 and v < 2:
                    pass
                elif v < 2:
                    filled(act, qx_in, qx_in_sw, i - 1, v + 2, NQ_SP, NQ_POOL)
                else:
                    filled(act, qx_in, qx_in_sw, i, v - 2, NQ_SP, NQ_POOL)
                for h in range(2):
                    cols = slice(HALF * h, HALF * h + HALF)
                    act.wait_ge(q_proj, cnt(i, v, 2, h + 1))
                    act.activation(q_src[u][:, 1, cols], pj[h][:, 0:HALF], ACT.Identity,
                                   bias=bias[:, 0:1]).then_inc(q_hi, 1)

            def exps(i, v, j):
                t = 7 * v + j
                act.wait_ge(st_done, i * 28 + t + 1)
                wait(act, pv_done, i * 28 + t - 3)
                act.activation(prob[t % 4][:, :, 0:L], st_ps[t % 2][:, 0:S8].rearrange("p (s q) -> p s q", q=L),
                               ACT.Exp).then_inc(exp_done, 1)

            def first():
                act.wait_ge(unit, 1)
                for t in (*q_unit, *k_unit):
                    act.activation(lines(t)[64:120], ident[64:120, 64:120].unsqueeze(1).to_broadcast([56, LINES, L]),
                                   ACT.Copy).then_inc(eyes, 1)
                act.wait_ge(weights, 1)
                for v in range(2):
                    high_k(0, v)
                    high_q(0, v)
                act.wait_ge(mask_in, 16 * 4)
                for v in range(2):
                    act.wait_ge(x_clear, 2 * v + 1)
                    for s in range(NH):
                        act.activation(lines(kx[v][64:120, s, :]), mask_f[64:120, s:s + 1, :].to_broadcast([56, LINES, L]),
                                       ACT.Copy).then_inc(x_mask, 1)

            def body(i, v, more_s, more_p):
                n2 = nxt(i, v, 2)
                for j in range(PAIRS):
                    exps(i, v, j)
                    if more_p and j == 0:
                        high_k(*n2)
                    if more_p and j == 1:
                        high_q(*n2)

            loop(act, body, first)

        @block.vector
        def _(dve):
            def low_k(i, v):
                for h in range(2):
                    cols = slice(HALF * h, HALF * h + HALF)
                    dve.wait_ge(k_hi, cnt(i, v, 2, h + 1))
                    dve.scalar_tensor_tensor(k_hilo[v][64:128, cols], pj[h][64:128, 0:HALF], bias[64:128, 1:2],
                                             k_hilo[v][64:128, cols], ALU.add, ALU.subtract).then_inc(k_lo, 1)
                dve.tensor_copy(k_unit[v][0:64, :], k_hilo[v][0:64, :]).then_inc(k_cp, 1)

            def low_q(i, v):
                u = v % 2
                for h in range(2):
                    cols = slice(HALF * h, HALF * h + HALF)
                    dve.wait_ge(q_hi, cnt(i, v, 2, h + 1))
                    dve.scalar_tensor_tensor(q_src[u][0:64, 0, cols], pj[h][0:64, 0:HALF], bias[0:64, 0:1],
                                             q_src[u][0:64, 1, cols], ALU.add, ALU.subtract).then_inc(q_lo, 1)
                wait(dve, q_lo, cnt(i, v, 2, 2))
                wait(dve, s_done, cnt(i, v, 7, -7))
                dve.tensor_copy(q_unit[u][0:64, :], q_src[u][0:64, 1, :]).then_inc(q_cp, 1)

            def values(i, v):
                u = v % 2
                wait(dve, vx_done, cnt(i, v, 4, -4))
                if isinstance(i, int):
                    wait(dve, v_io[u], i * 64 + (v // 2) * 32)
                else:
                    dve.wait_ge(v_io[u], i * 64 + (v // 2) * 32)
                dve.wait_ge(v_proj, cnt(i, v, 1, 1))
                dve.tensor_tensor(vf[u][:, :].rearrange("p (j c) -> p j c", c=C),
                                  pj[0][:, 0:PAIRS * C].rearrange("p (j c) -> p j c", c=C),
                                  bv[:, :].unsqueeze(1).to_broadcast([128, PAIRS, C]), ALU.add).then_inc(v_sb, 1)

            def line_max(i, v, j):
                dve.wait_ge(s_done, cnt(i, v, 7, j + 1))
                if j == 0:
                    wait(dve, mt_done, cnt(i, v, 1, -1))
                dve.tensor_reduce(mm[v % 2][:, 64 + NH * j:72 + NH * j],
                                  s_ps[j % 2][:, 0:S8].rearrange("p (s k) -> p s k", k=L),
                                  AX.X, ALU.max).then_inc(max_done, 1)

            def spread_max(i, v):
                u = v % 2
                dve.wait_ge(mt_done, cnt(i, v, 1, 1))
                wait(dve, st_done, cnt(i, v, 7, -7))
                for r in range(2):
                    dve.tensor_tensor(mx[u][64:120, r, :, :],
                                      s_ps[1][64:120, 64 * r:64 * r + L].unsqueeze(1).to_broadcast([56, NH, L]),
                                      negd[64:120, :].unsqueeze(2).to_broadcast([56, NH, L]),
                                      ALU.mult).then_inc(mx_done, 1)

            def normalise(i, v, g):
                u, n = v % 2, min(3, PAIRS - 3 * g)
                b = (3 * v + g) % 2
                dve.wait_ge(pv_done, cnt(i, v, 7, 3 * g + n))
                if g == 0:
                    if isinstance(i, int):
                        wait(dve, o_out[u], i * 64 + (v // 2) * 32)
                    else:
                        dve.wait_ge(o_out[u], i * 64 + (v // 2) * 32)
                if g == 0:
                    wait(dve, norm_done, cnt(i, v, 6, 0))
                else:
                    wait(dve, norm_done, cnt(i, v, 6, 2 * g))
                o = o_sb[u][:, :, :, :].rearrange("p r j (a d) -> p (j a) r d", a=4)
                for h in range(2):
                    p = slice(64 * h, 64 * h + L)
                    got = pv_ps[b][p, 0:VW * n].rearrange("p (j i r d) -> p j i r d", i=2, r=2, d=9)[:, :, h]
                    sums = rec[b][p, 0:8 * n].rearrange("p (j r) -> p j r", r=2)
                    dve.reciprocal(sums, got[:, :, :, 8]).then_inc(rec_done, 1)
                for h in range(2):
                    p = slice(64 * h, 64 * h + L)
                    got = pv_ps[b][p, 0:VW * n].rearrange("p (j i r d) -> p j i r d", i=2, r=2, d=9)[:, :, h]
                    sums = rec[b][p, 0:8 * n].rearrange("p (j r) -> p j r", r=2)
                    dve.wait_ge(rec_done, i * 24 + (6 * v + 2 * g + h + 1))
                    dve.tensor_tensor(o[p, 12 * g:12 * g + 4 * n], got[:, :, :, 0:8],
                                      sums.unsqueeze(3).to_broadcast([L, 4 * n, 2, 8]), ALU.mult).then_inc(norm_done, 1)

            def first():
                for t in (*vx, *mx, *mm, *prob, *s_ps, *st_ps, pj[0], pick, *w2):
                    nd = len(t.shape)
                    a = t[(slice(None),) * nd]
                    if nd == 3:
                        a = a.rearrange("p a b -> p (a b)")
                    if nd == 4:
                        a = a.rearrange("p a b c -> p (a b c)")
                    if a.dtype == BF16:
                        a = a.bitcast(F32)
                    ins = dve.memset(a, 0.0)
                ins.then_inc(cleared, 1)
                dve.wait_ge(cleared, 1)
                dve.wait_ge(par, 16 * 15)
                step = [0]

                def done(ins):
                    step[0] += 1
                    ins.then_inc(prep, 1)

                def settled():
                    dve.wait_ge(prep, step[0])

                for n in range(2):
                    ins = dve.tensor_copy(wdup[n][:, :].rearrange("p (h c) -> p h c", h=2),
                                          wf[n][0:C, :].unsqueeze(1).to_broadcast([C, 2, C]))
                done(ins)
                done(dve.tensor_copy(b_wide[:, :], b_c[0:C, :].to_broadcast([C, 128])))
                for n in range(3):
                    done(dve.tensor_scalar(wg[n][:, :], wf[n][:, :], g_c[:, 0:1], SCALE if n == 1 else 1.0,
                                           ALU.mult, ALU.mult))
                settled()
                for n in range(3):
                    done(dve.tensor_copy(w1[n][:, :].rearrange("p (h c) -> p h c", h=2),
                                         wg[n][:, :].unsqueeze(1).to_broadcast([128, 2, C])))
                settled()
                for n in range(3):
                    done(dve.tensor_tensor(w2[n][0:64, :].rearrange("p (h c) -> p h c", h=2),
                                           wg[n][0:64, :].unsqueeze(1).to_broadcast([64, 2, C]),
                                           w1[n][0:64, :].rearrange("p (h c) -> p h c", h=2), ALU.subtract))
                dve.wait_ge(pre_pe, 1)
                done(dve.tensor_tensor(bias[:, :], s_ps[1][:, 0:2], b_in[:, :], ALU.add))
                done(dve.tensor_tensor(bv[:, :], s_ps[1][:, C:2 * C], bv_in[:, :], ALU.add))
                settled()
                done(dve.tensor_scalar(bias[:, 1:2], bias[:, 1:2], SCALE, None, ALU.mult))
                settled()
                dve.sem_inc(weights, 1)
                for v in range(4):
                    d = vx[v][:, 0:PAIRS * VW].rearrange("p (j r d) -> p j r d", r=2, d=9)
                    for r in range(2):
                        done(dve.memset(d[64 * r:64 * r + L, :, r, 8:9], 1.0))
                settled()
                dve.sem_inc(ones_set, 1)
                dve.wait_ge(unit, 1)
                eye = ident[64:120, 64:120]
                done(dve.tensor_copy(pick[0:L], ident[0:L, 0:L].unsqueeze(1).to_broadcast([L, PAIRS, L])))
                done(dve.tensor_reduce(sel7[64:120, :], eye.rearrange("p (j s) -> p j s", s=NH), AX.X, ALU.add))
                done(dve.tensor_reduce(negd[64:120, :], eye.rearrange("p (j s) -> p s j", s=NH), AX.X, ALU.add,
                                       negate=True))
                settled()
                done(dve.tensor_copy(pick[64:120], sel7[64:120, :].unsqueeze(2).to_broadcast([56, PAIRS, L])))
                low_k(0, 0)
                dve.wait_ge(pre_pe, 2)
                mt = s_ps[0][:, 0:S8].rearrange("p (s q) -> p s q", q=L)
                done(dve.tensor_copy(mlo_hi[64:120], mt[64:120]))
                settled()
                done(dve.tensor_tensor(mlo[64:120], mt[64:120], mlo_hi[64:120], ALU.subtract))
                settled()
                for v in range(2):
                    if v:
                        low_k(0, v)
                    low_q(0, v)
                    if rows:
                        values(0, v)
                    for r in range(2):
                        done(dve.tensor_copy(mx[v][0:L, r, :, :], mt[0:L]))

                def mask_q(u):
                    dve.wait_ge(x_clear, 2 * u + 2)
                    for s in range(NH):
                        done(dve.tensor_copy(lines(qx[u][64:120, 0, s, :]),
                                             mlo[64:120, s:s + 1, :].to_broadcast([56, LINES, L])))
                    settled()
                    dve.sem_inc(ready, 1)

                mask_q(0)
                mask_q(1)
                for j in range(PAIRS):
                    line_max(0, 0, j)
                spread_max(0, 0)

            def body(i, v, more_s, more_p):
                n1, n2 = nxt(i, v, 1), nxt(i, v, 2)
                for j in range(PAIRS):
                    if j == 0 and not (isinstance(i, int) and i == 0 and v == 0):
                        normalise(*(nxt(i, v, -1) if v else (i - 1, 3)), 2)
                    if more_s and AHEAD[j]:
                        line_max(*n1, AHEAD[j][0])
                    if more_p and j == 0:
                        low_k(*n2)
                    if more_s:
                        for m in AHEAD[j][1:]:
                            line_max(*n1, m)
                        if j == MAXIMA_AT:
                            spread_max(*n1)
                    if more_p and j == 1:
                        low_q(*n2)
                    if j == 3:
                        normalise(i, v, 0)
                        if rows and more_p:
                            values(*n2)
                    if j == 6:
                        normalise(i, v, 1)

            loop(dve, body, first)
            normalise(B - 1, 3, 2)


NB4 = 4
NBATCH = B // NB4
J = H // 2
P2 = 2 * W


def conv_phase(nc, tag, pos, src_d, taps_d, bias_d, add_d, x1_d, xr_d, xc_d):
    R = 1 if pos else 2
    D = 2 * R + 1
    with ExitStack() as ctx:
        al = Alloc(nc, ctx, tag)
        sb, sem = al.sb, al.sem
        T = sb("taps", [128, 3, P2, C], F32)
        X = [sb(f"x{u}", [128, NB4, J + 2, C], F32) for u in range(2)]
        hl = [sb(f"hl{u}", [P2, J, 2 * C], BF16) for u in range(2)]
        xrt = [sb(f"xrt{u}", [128, G, CW], BF16) for u in range(2)]
        if pos:
            xc = [sb(f"xc{u}", [P2, J, C], F32) for u in range(2)]
            sq = sb("sq", [P2, J, C], F32)
            xct = sb("xct", [128, W, H], BF16)
            st = [sb(f"st{u}", [P2, 4, J], F32) for u in range(2)]
            half = sb("half", [P2, J], F32)
        else:
            add = [sb(f"add{u}", [P2, J, C], F32) for u in range(3)]
        tap_f = sb("tap_f", [96, C], F32)
        rest = [sb(f"rest{u}", [96, C], F32) for u in range(2)]
        part = [sb(f"part{u}", [96, C], BF16) for u in range(3)]
        tap3 = sb("tap3", [96, C], BF16)
        middle = sb("middle", [96, 1], F32)
        diag = sb("diag", [96, 6, 2, D], F32)
        pick = sb("pick", [96, 6, 3 * W], BF16)
        edge = sb("edge", [96, 6, 4, P2], BF16)
        ident = sb("ident", [128, 128], F32)
        ident_b = sb("ident_b", [128, 128], BF16)
        cv_ps = [al.ps(f"cv_ps{u}", [128, 512], F32) for u in range(4)]
        tr_ps = [al.ps(f"tr_ps{u}", [128, 1024], BF16) for u in range(4)]

        zeroed, unit = sem("zeroed"), sem("unit")
        taps_zero, taps_in, bias_in = sem("taps_zero"), sem("taps_in"), sem("bias_in")
        select_zero, selected = sem("select_zero"), sem("selected")
        ones_set, framed = sem("ones_set"), sem("framed")
        split = sem("split")
        pick_zero, pick_done = sem("pick_zero"), sem("pick_done")
        band_done = sem("band_done")
        band_act, band_dve = sem("band_act"), sem("band_dve")
        x_in = [sem(f"x_in{u}") for u in range(2)]
        add_in = [sem(f"add_in{u}") for u in range(3)]
        added = sem("added")
        id_done = sem("id_done")
        conv_done = sem("conv_done")
        conv_out = sem("conv_out")
        tr_done = sem("tr_done")
        xr_sb, xc_sb = sem("xr_sb"), sem("xc_sb")
        mean_in, mean_sb, xc_done = sem("mean_in"), sem("mean_sb"), sem("xc_done")
        sq_done, var_in, var_sb, rs_done = sem("sq_done"), sem("var_in"), sem("var_sb"), sem("rs_done")
        xn_done, hi_done, lo_done = sem("xn_done"), sem("hi_done"), sem("lo_done")
        half_done = sem("half_done")
        x1_out = [sem(f"x1_out{q}") for q in range(NB4)]
        xr_out = [sem(f"xr_out{u}") for u in range(2)]
        xc_out = sem("xc_out")

        def tokens(dram, b):
            return dram[b].rearrange("(j r) w c -> (r w) j c", r=2)

        images = [(b, q) for b in range(NBATCH) for q in range(NB4)]
        SPLIT_STEPS = 9
        EDGES = (0, 1, W - 2, W - 1)
        block = ctx.enter_context(nc.Block())

        @block.sync
        def _(sp):
            def load(b, q):
                u = b % 2
                if b >= 2:
                    n = NB4 * (b - 2) + q
                    if pos:
                        sp.wait_ge(xc_done, n + 1)
                        sp.wait_ge(x1_out[q], 16 * (b - 1))
                    else:
                        sp.wait_ge(lo_done, n + 1)
                        sp.wait_ge(hi_done, n + 1)
                sp.dma_start(X[u][0:P2, q, 1:J + 1, :], tokens(src_d, NB4 * b + q)).then_inc(x_in[u], 16)

            def load_add(n):
                if n >= 3:
                    sp.wait_ge(added, n - 2)
                sp.dma_start(add[n % 3][:, :, :], tokens(add_d, n)).then_inc(add_in[n % 3], 16)

            LAG = 3

            def store_t(n):
                sp.wait_ge(xr_sb, G * (n + 1))
                sp.dma_start(xr_d[G * n:G * n + G].rearrange("g p t -> p g t"), xrt[n % 2][:, :, :]).then_inc(
                    xr_out[n % 2], 16)
                if pos:
                    sp.wait_ge(xc_sb, G * (n + 1))
                    sp.dma_start(xc_d[G * n:G * n + G].rearrange("g p t -> p g t"),
                                 xct[:, :, :].rearrange("p (g l) h -> p g (l h)", g=G)).then_inc(xc_out, 16)

            sp.wait_ge(taps_zero, 1)
            for k in range(3):
                sp.dma_start(tap_f[32 * k:32 * k + D * D, :], taps_d.rearrange("a b c -> (a b) c")).then_inc(taps_in, 16)
            src = bass.AP(bias_d.tensor, bias_d.offset, [[C, 1], [0, P2], [1, C]])
            sp.dma_start(T[P2:P2 + 1, 1, :, :], src).then_inc(bias_in, 16)
            for b in range(2):
                sp.wait_ge(framed, b + 1)
                for q in range(NB4):
                    load(b, q)
            if not pos:
                for n in range(3):
                    load_add(n)
            for n, (b, q) in enumerate(images):
                if pos:
                    sp.wait_ge(conv_out, 16 * (b + 1))
                    sp.dma_start(tokens(x1_d, n), X[b % 2][0:P2, q, 1:J + 1, :]).then_inc(x1_out[q], 16)
                elif n and n + 2 < B:
                    load_add(n + 2)
                if n >= LAG:
                    store_t(n - LAG)
                if n and images[n - 1][0] + 2 < NBATCH:
                    load(images[n - 1][0] + 2, images[n - 1][1])
            for n in range(B - LAG, B):
                store_t(n)
            for u in range(2):
                sp.wait_ge(xr_out[u], 16 * B // 2)
            if pos:
                sp.wait_ge(xc_out, 16 * B)
                for q in range(NB4):
                    sp.wait_ge(x1_out[q], 16 * NBATCH)

        BANKS = [(d, r2, w) for d in range(3) for r2 in range(2) for w in range(0, W, 8)]

        def bank_out(eng, copy, n, done):
            d, r2, w = BANKS[n]
            eng.wait_ge(band_done, n + 1)
            copy(T[0:P2, d, W * r2 + w:W * r2 + w + 8, :],
                 cv_ps[n % 4][0:P2, :].rearrange("p (w c) -> p w c", c=C)).then_inc(done, 1)

        @block.gpsimd
        def _(pool):
            pool.memset(diag[:, :, :, :].rearrange("p s r z -> p (s r z)"), 0.0)
            pool.memset(middle[:, :], 0.0).then_inc(select_zero, 1)
            pool.wait_ge(select_zero, 1)
            for k in range(3):
                pool.affine_select(out=diag[:, :, :, :], in_=diag[:, :, :, :], compare_op=ALU.not_equal, fill=1.0,
                                   base=-32 * k - D * (R - 3), pattern=[[-D, 6], [-D, 2], [-1, D]],
                                   channel_multiplier=1).then_inc(select_zero, 1)
                pool.affine_select(out=middle[:, :], in_=middle[:, :], compare_op=ALU.not_equal, fill=1.0,
                                   base=-32 * k - R * D - R, pattern=[[0, 1]], channel_multiplier=1).then_inc(select_zero, 1)
                pool.wait_ge(select_zero, 2 * k + 3)
            pool.sem_inc(selected, 1)
            for u in range(2):
                pool.memset(X[u][96:128].rearrange("p n j c -> p (n j c)"), 1.0).then_inc(ones_set, 1)
                pool.wait_ge(ones_set, u + 1)
                pool.memset(X[u][:, :, 0:J + 2:J + 1, :], 0.0).then_inc(framed, 1)
                if u == 0:
                    identity_on(pool, ident, zeroed, unit)
                    pool.wait_ge(unit, 1)
            if pos:
                pool.memset(half[:, :], -0.5).then_inc(half_done, 1)
                pool.wait_ge(half_done, 1)
            for n, (b, q) in enumerate(images):
                u = n % 2
                if pos:
                    def lo(n):
                        u = n % 2
                        pool.wait_ge(hi_done, n + 1)
                        if n >= 2:
                            pool.wait_ge(tr_done, G * (n - 1))
                        pool.tensor_tensor(hl[u][:, :, C:2 * C], xc[u][:, :, :], hl[u][:, :, 0:C],
                                           ALU.subtract).then_inc(lo_done, 1)
                    if n:
                        lo(n - 1)
                    pool.wait_ge(var_sb, n + 1)
                    pool.tensor_tensor(st[u][:, 3, :], st[u][:, 2, :], half[:, :], ALU.pow).then_inc(rs_done, 1)
                    if n == B - 1:
                        lo(n)
                else:
                    pool.wait_ge(hi_done, n + 1)
                    if n >= 2:
                        pool.wait_ge(tr_done, G * (n - 1))
                    pool.tensor_tensor(hl[u][:, :, C:2 * C], X[b % 2][0:P2, q, 1:J + 1, :], hl[u][:, :, 0:C],
                                       ALU.subtract).then_inc(lo_done, 1)

        @block.tensor
        def _(pe):
            def conv(b, cg):
                u, t = b % 2, 16 * b + cg
                if cg == 0:
                    pe.wait_ge(framed, u + 1)
                    pe.wait_ge(x_in[u], 16 * NB4 * (b // 2 + 1))
                if t >= 4:
                    pe.wait_ge(conv_out, t - 3)
                for k in range(4):
                    c = 4 * cg + k
                    for d in (1, 0, 2):
                        kp = P2 + 1 if d == 1 else P2
                        ins = pe.matmul(cv_ps[t % 4][0:P2, P2 * k:P2 * k + P2].rearrange("p (n j) -> p n j", j=J),
                                        T[0:kp, d, :, c], X[u][0:kp, :, d:d + J, c], start=d == 1, stop=d == 2)
                ins.then_inc(conv_done, 1)

            pe.wait_ge(split, SPLIT_STEPS)
            pe.wait_ge(pick_done, 2)
            for n, (d, r2, w) in enumerate(BANKS):
                if n >= 4:
                    pe.wait_ge(band_act if n % 2 == 0 else band_dve, n // 2 - 1)
                for k in range(8):
                    s = 2 * d - r2 + 1
                    rows = edge[:, s, EDGES.index(w + k), :] if w + k in EDGES else \
                        pick[:, s, W - w - k:3 * W - w - k]
                    ins = pe.matmul(cv_ps[n % 4][0:P2, C * k:C * k + C], rows, tap3[:, :], start=True, stop=True)
                ins.then_inc(band_done, 1)
            pe.wait_ge(band_act, len(BANKS) // 2)
            pe.wait_ge(band_dve, len(BANKS) // 2)
            pe.wait_ge(bias_in, 16)
            pe.wait_ge(framed, 1)
            pe.wait_ge(id_done, 1)
            for cg in range(16):
                conv(0, cg)
            def transposes(n):
                pe.wait_ge(lo_done, n + 1)
                for g in range(G):
                    t = G * n + g
                    if t >= 4:
                        pe.wait_ge(xr_sb, t - 3)
                        if pos:
                            pe.wait_ge(xc_sb, t - 3)
                    for j in range(PAIRS):
                        ins = pe.transpose(tr_ps[t % 4][:, P2 * j:P2 * j + P2], hl[n % 2][:, PAIRS * g + j, :],
                                           ident_b[0:P2, 0:P2])
                    ins.then_inc(tr_done, 1)

            for n, (b, q) in enumerate(images):
                if b + 1 < NBATCH:
                    for cg in range(4):
                        conv(b + 1, 4 * q + cg)
                if n:
                    transposes(n - 1)
            transposes(B - 1)

        @block.scalar
        def _(act):
            def conv_copy(b, cg):
                t = 16 * b + cg
                act.wait_ge(conv_done, t + 1)
                act.activation(X[b % 2][0:P2, :, 1:J + 1, 4 * cg:4 * cg + 4].rearrange("p n j c -> p c n j"),
                               cv_ps[t % 4][0:P2, 0:4 * P2].rearrange("p (c n j) -> p c n j", c=4, j=J),
                               ACT.Copy).then_inc(conv_out, 1)

            def high(n):
                b, q = images[n]
                if pos:
                    act.wait_ge(xn_done, n + 1)
                else:
                    act.wait_ge(added, n + 1)
                if n >= 2:
                    act.wait_ge(tr_done, G * (n - 1))
                src = xc[n % 2][:, :, :] if pos else X[b % 2][0:P2, q, 1:J + 1, :]
                act.activation(hl[n % 2][:, :, 0:C], src, ACT.Copy).then_inc(hi_done, 1)

            def row_copy(n):
                if n >= 2:
                    act.wait_ge(xr_out[n % 2], 16 * (n // 2))
                for g in range(G):
                    act.wait_ge(tr_done, G * n + g + 1)
                    act.activation(xrt[n % 2][:, g, :], tr_ps[(G * n + g) % 4][:, 0:CW],
                                   ACT.Copy).then_inc(xr_sb, 1)

            act.wait_ge(unit, 1)
            act.activation(ident_b[:, :], ident[:, :], ACT.Copy).then_inc(id_done, 1)
            for n in range(0, len(BANKS), 2):
                bank_out(act, lambda o, i: act.activation(o, i, ACT.Copy), n, band_act)
            for cg in range(16):
                conv_copy(0, cg)
            for n, (b, q) in enumerate(images):
                if n >= 2:
                    row_copy(n - 2)
                if pos:
                    act.wait_ge(xc_done, n + 1)
                    if n:
                        act.wait_ge(var_in, n)
                    act.activation(sq[:, :, :], xc[n % 2][:, :, :], ACT.Square).then_inc(sq_done, 1)
                    if n:
                        high(n - 1)
                else:
                    high(n)
                if b + 1 < NBATCH:
                    for cg in range(4):
                        conv_copy(b + 1, 4 * q + cg)
            if pos:
                high(B - 1)
            row_copy(B - 2)
            row_copy(B - 1)

        @block.vector
        def _(dve):
            def add_attention(n):
                b, q = images[n]
                x = X[b % 2][0:P2, q, 1:J + 1, :]
                dve.wait_ge(conv_out, 16 * (b + 1))
                dve.wait_ge(add_in[n % 3], 16 * (n // 3 + 1))
                dve.tensor_tensor(x, x, add[n % 3][:, :, :], ALU.add).then_inc(added, 1)

            def center(n):
                b, q = images[n]
                u, x1 = n % 2, X[b % 2][0:P2, q, 1:J + 1, :]
                dve.wait_ge(conv_out, 16 * (b + 1))
                if n >= 2:
                    dve.wait_ge(rs_done, n - 1)
                dve.tensor_reduce(st[u][:, 0, :], x1, AX.X, ALU.add).then_inc(mean_in, 1)
                dve.wait_ge(mean_in, n + 1)
                dve.tensor_scalar(st[u][:, 1, :], st[u][:, 0, :], -1.0 / C, None, ALU.mult).then_inc(mean_sb, 1)
                dve.wait_ge(mean_sb, n + 1)
                if n >= 2:
                    dve.wait_ge(lo_done, n - 1)
                    dve.wait_ge(hi_done, n - 1)
                dve.tensor_tensor(xc[u][:, :, :], x1, st[u][:, 1, :].unsqueeze(2).to_broadcast([P2, J, C]),
                                  ALU.add).then_inc(xc_done, 1)

            def variance(n):
                u = n % 2
                dve.wait_ge(sq_done, n + 1)
                dve.tensor_reduce(st[u][:, 0, :], sq[:, :, :], AX.X, ALU.add).then_inc(var_in, 1)
                dve.wait_ge(var_in, n + 1)
                dve.tensor_scalar(st[u][:, 2, :], st[u][:, 0, :], 1.0 / C, EPS, ALU.mult, ALU.add).then_inc(var_sb, 1)

            def scale(n):
                u = n % 2
                dve.wait_ge(rs_done, n + 1)
                dve.tensor_tensor(xc[u][:, :, :], xc[u][:, :, :],
                                  st[u][:, 3, :].unsqueeze(2).to_broadcast([P2, J, C]), ALU.mult).then_inc(xn_done, 1)

            def col_copy(n, halves):
                for g in halves:
                    dve.wait_ge(tr_done, G * n + g + 1)
                    dve.wait_ge(xr_sb, G * n + g + 1)
                    if g == 0 and n:
                        dve.wait_ge(xc_out, 16 * n)
                    dve.tensor_copy(xct[:, :, LINES * g:LINES * g + LINES].rearrange("p w h -> p h w"),
                                    tr_ps[(G * n + g) % 4][:, 0:CW].rearrange("p (h w) -> p h w", w=W)).then_inc(xc_sb, 1)

            dve.memset(tap_f[:, :], 0.0).then_inc(taps_zero, 1)
            dve.memset(pick[:, :, :].rearrange("p s z -> p (s z)"), 0.0).then_inc(pick_zero, 1)
            dve.wait_ge(pick_zero, 1)
            dve.wait_ge(selected, 1)
            dve.tensor_copy(pick[:, :, :].rearrange("p s (z w) -> p s z w", w=W)[:, :, 1:3, 0:R + 1],
                            diag[:, :, :, R:D]).then_inc(pick_zero, 1)
            dve.tensor_copy(pick[:, :, :].rearrange("p s (z w) -> p s z w", w=W)[:, :, 0:2, W - R:W],
                            diag[:, :, :, 0:R]).then_inc(pick_zero, 1)
            dve.wait_ge(pick_zero, 3)
            for e, w in enumerate(EDGES):
                dve.tensor_copy(edge[:, :, e, :], pick[:, :, W - w:3 * W - w]).then_inc(pick_zero, 1)
            dve.wait_ge(pick_zero, 3 + len(EDGES))
            for e, w in enumerate(EDGES):
                low, high = min(w - R, 0), max(w + R - W + 1, 0)
                if low or high:
                    ins = dve.memset(edge[:, :, e, W + low:W + high], 0.0)
            ins.then_inc(pick_done, 2)
            dve.wait_ge(taps_in, 48)
            if pos:
                dve.tensor_scalar(tap_f[:, :], tap_f[:, :], middle[:, 0:1], None, ALU.add).then_inc(split, 1)
            else:
                dve.sem_inc(split, 1)
            dve.wait_ge(split, 1)
            dve.tensor_copy(part[0][:, :], tap_f[:, :]).then_inc(split, 1)
            dve.wait_ge(split, 2)
            dve.tensor_tensor(rest[0][:, :], tap_f[:, :], part[0][:, :], ALU.subtract).then_inc(split, 1)
            dve.wait_ge(split, 3)
            dve.tensor_copy(part[1][:, :], rest[0][:, :]).then_inc(split, 1)
            dve.wait_ge(split, 4)
            dve.tensor_tensor(rest[1][:, :], rest[0][:, :], part[1][:, :], ALU.subtract).then_inc(split, 1)
            dve.wait_ge(split, 5)
            dve.tensor_copy(part[2][:, :], rest[1][:, :]).then_inc(split, 1)
            dve.wait_ge(split, 6)
            for k in range(3):
                rows = slice(32 * k, 32 * k + 32)
                dve.tensor_copy(tap3[rows, :], part[k][rows, :]).then_inc(split, 1)
            for n in range(1, len(BANKS), 2):
                bank_out(dve, dve.tensor_copy, n, band_dve)
            for n, (b, q) in enumerate(images):
                if pos:
                    center(n)
                    if n:
                        scale(n - 1)
                    if n >= 2:
                        col_copy(n - 2, range(0, 2))
                    variance(n)
                    if n >= 2:
                        col_copy(n - 2, range(2, G))
                else:
                    add_attention(n)
            if pos:
                scale(B - 1)
                col_copy(B - 2, range(G))
                col_copy(B - 1, range(G))


def mlp_phase(nc, tag, rt_d, x1_d, wo_d, bo_d, ln_g, ln_b, wf1_d, bf1_d, wf2_d, bf2_d, out_d):
    STREAM = 96
    with ExitStack() as ctx:
        al = Alloc(nc, ctx, tag)
        sb, sem = al.sb, al.sem
        rt = [sb(f"rt{u}", [128, CW], BF16) for u in range(2)] * 2
        x1 = [sb(f"x1{u}", [P2, PAIRS, C], F32) for u in range(2)] * 2
        x2 = [sb(f"x2{u}", [P2, PAIRS, C], F32) for u in range(4)]
        xc = [sb(f"xc{u}", [P2, PAIRS, C], F32) for u in range(2)] * 2
        sq = [sb(f"sq{u}", [P2, PAIRS, C], F32) for u in range(2)] * 2
        st = [sb(f"st{u}", [P2, 5, PAIRS], F32) for u in range(2)] * 2
        hl = [sb(f"hl{u}", [P2, PAIRS, 2 * C], BF16) for u in range(2)] * 2
        yt = [sb(f"yt{u}", [128, CW], BF16) for u in range(2)] * 2
        ht = [sb(f"ht{u}", [128, 2, CW], F32) for u in range(2)] * 2
        o_sb = [sb(f"o{u}", [P2, PAIRS, C], F32) for u in range(2)] * 2
        half = sb("half", [P2, PAIRS], F32)
        ident = sb("ident", [128, 128], F32)
        ident_b = sb("ident_b", [128, 128], BF16)
        wo_f = sb("wo_f", [128, C], F32)
        wo1 = sb("wo1", [128, C], BF16)
        wo2 = sb("wo2", [128, C], BF16)
        w1_f = sb("w1_f", [128, FF], F32)
        w1_g = sb("w1_g", [128, FF], F32)
        w11 = sb("w11", [128, FF], BF16)
        w12 = sb("w12", [128, FF], BF16)
        w2_p = sb("w2_p", [128, 2, STREAM], F32)
        g_c = sb("g_c", [128, 1], F32)
        b_c = sb("b_c", [128, 1], F32)
        b1_in = sb("b1_in", [128, 2], F32)
        b1 = sb("b1", [128, 2], F32)
        bo = sb("bo", [P2, C], F32)
        b2 = sb("b2", [P2, C], F32)

        o_ps = [al.ps(f"o_ps{u}", [128, 512], F32) for u in range(2)] * 2
        t_ps = [al.ps(f"t_ps{u}", [128, 1024], BF16) for u in range(2)] * 2
        h_ps = [al.ps(f"h_ps{u}", [128, 512], F32) for u in range(2)]
        y_ps = [al.ps(f"y_ps{u}", [128, 512], F32) for u in range(2)]

        par, zeroed, unit, prep, pre_pe, ready, half_done = (
            sem(n) for n in ("par", "zeroed", "unit", "prep", "pre_pe", "ready", "half_done"))
        rt_in = [sem(f"rt_in{u}") for u in range(2)] * 2
        x1_in = [sem(f"x1_in{u}") for u in range(2)] * 2
        out_st = [sem(f"out_st{u}") for u in range(2)] * 2
        x1b_done, rs_done, lo_done, x2b_done = (sem(n) for n in ("x1b_done", "rs_done", "lo_done", "x2b_done"))
        o_done, t_done, fc1_done, fc2_done = (sem(n) for n in ("o_done", "t_done", "fc1_done", "fc2_done"))
        sq_done, hi_done, yt_done, gelu_done = (sem(n) for n in ("sq_done", "hi_done", "yt_done", "gelu_done"))
        x2_done, mean_in, mean_sb, xc_done = (sem(n) for n in ("x2_done", "mean_in", "mean_sb", "xc_done"))
        var_in, var_sb, xn_done, out_sb = (sem(n) for n in ("var_in", "var_sb", "xn_done", "out_sb"))

        passed = {mybir.EngineType.Pool: sem("passed_pool"), mybir.EngineType.SP: sem("passed_sp")}

        def cnt(i, v, per, plus):
            return i * (4 * per) + (v * per + plus)

        def chunk(i, v, d):
            return i + (v + d) // 4, (v + d) % 4

        def use(i, v, plus):
            return i * 32 + (v // 2 + plus) * 16

        def wait(eng, s, val):
            if not isinstance(val, int):
                eng.wait_ge(s, val)
                if eng.engine in passed:
                    eng.sem_inc(passed[eng.engine], 1)
            elif val > 0:
                eng.wait_ge(s, val)

        NI = NCH // 4

        def loop(eng, body):
            for v in range(4):
                body(0, v, v > 0, 4)
            with eng.Fori(1, NI - 1) as i:
                for v in range(4):
                    body(i, v, True, 4)
            for v in range(4):
                body(NI - 1, v, True, 3 - v)

        x1_v = x1_d.rearrange("b (g j r) w c -> (b g) (r w) j c", g=G, r=2)
        out_v = out_d.rearrange("b (g j r) w c -> (b g) (r w) j c", g=G, r=2)
        block = ctx.enter_context(nc.Block())

        @block.sync
        def _(sp):
            def load(i, v):
                wait(sp, o_done, cnt(i, v, 1, -1))
                sp.dma_start(rt[v][:, :], rt_d[4 * i + v]).then_inc(rt_in[v], 16)
                wait(sp, x2_done, cnt(i, v, 1, -1))
                sp.dma_start(x1[v][:, :, :], x1_v[4 * i + v]).then_inc(x1_in[v], 16)

            def store(i, v):
                wait(sp, out_sb, cnt(i, v, 2, 2))
                sp.dma_start(out_v[4 * i + v], o_sb[v][:, :, :]).then_inc(out_st[v], 16)

            for h in range(2):
                p = slice(64 * h, 64 * h + 64)
                sp.dma_start(wo_f[p, :], wo_d).then_inc(par, 16)
                sp.dma_start(w1_f[p, :], wf1_d).then_inc(par, 16)
                sp.dma_start(g_c[p, :], ln_g.unsqueeze(1)).then_inc(par, 16)
                sp.dma_start(b_c[p, :], ln_b.unsqueeze(1)).then_inc(par, 16)
                sp.dma_start(w2_p[:, h, 0:C], wf2_d[128 * h:128 * h + 128, :]).then_inc(par, 16)
                sp.dma_start(b1_in[:, h:h + 1], bf1_d[128 * h:128 * h + 128].unsqueeze(1)).then_inc(par, 16)
            sp.dma_start(bo[:, :], bo_d.partition_broadcast(P2)).then_inc(par, 16)
            sp.dma_start(b2[:, :], bf2_d.partition_broadcast(P2)).then_inc(par, 16)
            load(0, 0)
            load(0, 1)
            load(0, 2)
            load(0, 3)

            def body(i, v, before, after):
                if after >= 4:
                    load(*chunk(i, v, 4))
                if before:
                    store(*chunk(i, v, -1))

            loop(sp, body)
            store(NI - 1, 3)
            for v in range(2):
                sp.wait_ge(out_st[v], 32 * NI)

        @block.gpsimd
        def _(pool):
            def bias_o(i, v):
                wait(pool, x1_in[v], use(i, v, 1))
                pool.tensor_tensor(x1[v][:, :, :], x1[v][:, :, :], bo[:, :].unsqueeze(1).to_broadcast([P2, PAIRS, C]),
                                   ALU.add).then_inc(x1b_done, 1)

            def deviation(i, v):
                wait(pool, var_sb, cnt(i, v, 1, 1))
                pool.tensor_tensor(st[v][:, 4, :], st[v][:, 3, :], half[:, :], ALU.pow).then_inc(rs_done, 1)

            def low(i, v):
                wait(pool, hi_done, cnt(i, v, 1, 1))
                pool.tensor_tensor(hl[v][:, :, C:2 * C], xc[v][:, :, :], hl[v][:, :, 0:C],
                                   ALU.subtract).then_inc(lo_done, 1)

            def bias_2(i, v):
                wait(pool, xc_done, cnt(i, v, 1, 1))
                pool.tensor_tensor(x2[v][:, :, :], x2[v][:, :, :], b2[:, :].unsqueeze(1).to_broadcast([P2, PAIRS, C]),
                                   ALU.add).then_inc(x2b_done, 1)

            identity_on(pool, ident, zeroed, unit)
            pool.memset(half[:, :], -0.5).then_inc(half_done, 1)
            pool.wait_ge(half_done, 1)
            pool.wait_ge(par, 16 * 14)
            bias_o(0, 0)
            bias_o(0, 1)
            deviation(0, 0)
            low(0, 0)
            bias_2(0, 0)
            bias_o(0, 2)
            deviation(0, 1)

            def body(i, v, before, after):
                if after >= 1:
                    low(*chunk(i, v, 1))
                if after >= 3:
                    bias_o(*chunk(i, v, 3))
                if after >= 2:
                    deviation(*chunk(i, v, 2))
                if after >= 1:
                    bias_2(*chunk(i, v, 1))

            loop(pool, body)

        @block.tensor
        def _(pe):
            def project(i, v):
                pe.wait_ge(rt_in[v], use(i, v, 1))
                wait(pe, x2_done, cnt(i, v, 1, -1))
                for j in range(PAIRS):
                    for n, w in enumerate((wo1, wo2)):
                        ins = pe.matmul(o_ps[v][0:P2, C * j:C * j + C], rt[v][:, P2 * j:P2 * j + P2], w[:, :],
                                        start=n == 0, stop=n == 1)
                ins.then_inc(o_done, 1)

            def turn(i, v):
                pe.wait_ge(lo_done, cnt(i, v, 1, 1))
                wait(pe, yt_done, cnt(i, v, 1, -1))
                for j in range(PAIRS):
                    ins = pe.transpose(t_ps[v][:, P2 * j:P2 * j + P2], hl[v][:, j, :], ident_b[0:P2, 0:P2])
                ins.then_inc(t_done, 1)

            def fc1(i, v, h):
                pe.wait_ge(yt_done, cnt(i, v, 1, 1))
                for f in range(2):
                    wait(pe, gelu_done, cnt(i, v, 4, 2 * h + f - 1))
                    cols = slice(HALF * h, HALF * h + HALF)
                    pe.matmul(h_ps[f][:, 0:HALF], w11[:, 128 * f:128 * f + 128], yt[v][:, cols],
                              start=True, stop=False)
                    pe.matmul(h_ps[f][:, 0:HALF], w12[:, 128 * f:128 * f + 128], yt[v][:, cols],
                              start=False, stop=True).then_inc(fc1_done, 1)

            def fc2(i, v, n):
                pe.wait_ge(gelu_done, cnt(i, v, 4, 4))
                wait(pe, out_sb, cnt(i, v, 2, n - 1))
                for j in range(4 * n, min(4 * n + 4, PAIRS)):
                    for f in range(2):
                        ins = pe.matmul(y_ps[n][0:P2, 128 * (j % 4):128 * (j % 4) + STREAM],
                                        ht[v][:, f, P2 * j:P2 * j + P2], w2_p[:, f, :], start=f == 0, stop=f == 1)
                ins.then_inc(fc2_done, 1)

            pe.wait_ge(par, 16 * 14)
            for f in range(2):
                ins = pe.matmul(h_ps[0][:, f:f + 1], w1_f[0:C, 128 * f:128 * f + 128], b_c[0:C, :],
                                start=True, stop=True)
            ins.then_inc(pre_pe, 1)
            pe.wait_ge(ready, 1)
            project(0, 0)
            project(0, 1)

            def body(i, v, before, after):
                turn(i, v)
                if after >= 2:
                    project(*chunk(i, v, 2))
                for n in range(2):
                    if before:
                        fc2(*chunk(i, v, -1), n)
                    fc1(i, v, n)

            loop(pe, body)
            for n in range(2):
                fc2(NI - 1, 3, n)

        @block.scalar
        def _(act):
            def square(i, v):
                act.wait_ge(xc_done, cnt(i, v, 1, 1))
                wait(act, var_in, cnt(i, v, 1, -1))
                act.activation(sq[v][:, :, :], xc[v][:, :, :], ACT.Square).then_inc(sq_done, 1)

            def high(i, v):
                act.wait_ge(xn_done, cnt(i, v, 1, 1))
                wait(act, t_done, cnt(i, v, 1, -1))
                act.activation(hl[v][:, :, 0:C], xc[v][:, :, :], ACT.Copy).then_inc(hi_done, 1)

            act.wait_ge(ready, 1)
            square(0, 0)
            high(0, 0)
            square(0, 1)

            def body(i, v, before, after):
                act.wait_ge(t_done, cnt(i, v, 1, 1))
                wait(act, fc1_done, cnt(i, v, 4, -4))
                act.activation(yt[v][:, :], t_ps[v][:, 0:CW], ACT.Copy).then_inc(yt_done, 1)
                if after >= 1:
                    high(*chunk(i, v, 1))
                if after >= 2:
                    square(*chunk(i, v, 2))
                for h in range(2):
                    for f in range(2):
                        act.wait_ge(fc1_done, cnt(i, v, 4, 2 * h + f + 1))
                        wait(act, fc2_done, cnt(i, v, 2, -2))
                        act.activation(ht[v][:, f, HALF * h:HALF * h + HALF], h_ps[f][:, 0:HALF], ACT.Gelu,
                                       bias=b1[:, f:f + 1]).then_inc(gelu_done, 1)

            loop(act, body)

        @block.vector
        def _(dve):
            def front(i, v):
                dve.wait_ge(o_done, cnt(i, v, 1, 1))
                dve.wait_ge(x1b_done, cnt(i, v, 1, 1))
                wait(dve, out_sb, cnt(i, v, 2, -6))
                dve.tensor_tensor(x2[v][:, :, :], o_ps[v][0:P2, 0:PAIRS * C].rearrange("p (j c) -> p j c", c=C),
                                  x1[v][:, :, :], ALU.add).then_inc(x2_done, 1)
                dve.wait_ge(x2_done, cnt(i, v, 1, 1))
                dve.tensor_reduce(st[v][:, 0, :], x2[v][:, :, :], AX.X, ALU.add).then_inc(mean_in, 1)
                dve.wait_ge(mean_in, cnt(i, v, 1, 1))
                dve.tensor_scalar(st[v][:, 1, :], st[v][:, 0, :], -1.0 / C, None, ALU.mult).then_inc(mean_sb, 1)
                dve.wait_ge(mean_sb, cnt(i, v, 1, 1))
                wait(dve, lo_done, cnt(i, v, 1, -1))
                dve.tensor_tensor(xc[v][:, :, :], x2[v][:, :, :],
                                  st[v][:, 1, :].unsqueeze(2).to_broadcast([P2, PAIRS, C]), ALU.add).then_inc(xc_done, 1)

            def variance(i, v):
                dve.wait_ge(sq_done, cnt(i, v, 1, 1))
                dve.tensor_reduce(st[v][:, 2, :], sq[v][:, :, :], AX.X, ALU.add).then_inc(var_in, 1)
                dve.wait_ge(var_in, cnt(i, v, 1, 1))
                wait(dve, rs_done, cnt(i, v, 1, -1))
                dve.tensor_scalar(st[v][:, 3, :], st[v][:, 2, :], 1.0 / C, EPS, ALU.mult, ALU.add).then_inc(var_sb, 1)

            def scale(i, v):
                dve.wait_ge(rs_done, cnt(i, v, 1, 1))
                dve.tensor_tensor(xc[v][:, :, :], xc[v][:, :, :],
                                  st[v][:, 4, :].unsqueeze(2).to_broadcast([P2, PAIRS, C]), ALU.mult).then_inc(xn_done, 1)

            def result(i, v, n):
                if n == 0:
                    dve.wait_ge(x2b_done, cnt(i, v, 1, 1))
                    wait(dve, out_st[v], use(i, v, 0))
                a, b = 4 * n, min(4 * n + 4, PAIRS)
                dve.wait_ge(fc2_done, cnt(i, v, 2, n + 1))
                dve.tensor_tensor(o_sb[v][:, a:b, :],
                                  y_ps[n][0:P2, 0:128 * (b - a)].rearrange("p (j c) -> p j c", c=128)[:, :, 0:C],
                                  x2[v][:, a:b, :], ALU.add).then_inc(out_sb, 1)

            step = [0]

            def done(ins):
                step[0] += 1
                ins.then_inc(prep, 1)

            def settled():
                dve.wait_ge(prep, step[0])

            done(dve.memset(wo2[:, :], 0.0))
            done(dve.memset(w12[:, :], 0.0))
            done(dve.memset(w2_p[:, :, C:STREAM], 0.0))
            dve.wait_ge(par, 16 * 14)
            done(dve.tensor_copy(wo1[:, :], wo_f[:, :]))
            done(dve.tensor_scalar(w1_g[:, :], w1_f[:, :], g_c[:, 0:1], None, ALU.mult))
            settled()
            done(dve.tensor_tensor(wo2[0:64, :], wo_f[0:64, :], wo1[0:64, :], ALU.subtract))
            done(dve.tensor_copy(w11[:, :], w1_g[:, :]))
            settled()
            done(dve.tensor_tensor(w12[0:64, :], w1_g[0:64, :], w11[0:64, :], ALU.subtract))
            dve.wait_ge(pre_pe, 1)
            done(dve.tensor_tensor(b1[:, :], h_ps[0][:, 0:2], b1_in[:, :], ALU.add))
            dve.wait_ge(unit, 1)
            done(dve.tensor_copy(ident_b[:, :], ident[:, :]))
            settled()
            dve.sem_inc(ready, 1)
            front(0, 0)
            variance(0, 0)
            front(0, 1)
            scale(0, 0)
            variance(0, 1)

            def body(i, v, before, after):
                if after >= 1:
                    scale(*chunk(i, v, 1))
                if after >= 2:
                    front(*chunk(i, v, 2))
                if before:
                    result(*chunk(i, v, -1), 0)
                if after >= 2:
                    variance(*chunk(i, v, 2))
                if before:
                    result(*chunk(i, v, -1), 1)

            loop(dve, body)
            for n in range(2):
                result(NI - 1, 3, n)


def build(nc, x, mask_h, mask_w, pos_w, pos_b, ln1_g, ln1_b, q_w, q_b, k_w, k_b, v_w, v_b, lepe_w, lepe_b,
          out_w, out_b, ln2_g, ln2_b, fc1_w, fc1_b, fc2_w, fc2_b, out):
    def scratch(name, shape, dt):
        return nc.dram_tensor(name, shape, dt).ap()

    x1_d = scratch("x1_scratch", [B, H, W, C], F32)
    v_d = scratch("v_scratch", [B, H, W, C], F32)
    row_d = scratch("row_attention", [B, H, W, C], F32)
    att_d = scratch("attention", [B, H, W, C], F32)
    xr_d = scratch("xn_rows", [NCH, 128, CW], BF16)
    xc_d = scratch("xn_cols", [NCH, 128, CW], BF16)
    rt_d = scratch("r_rows", [NCH, 128, CW], BF16)
    qkv = [q_w, k_w, v_w], [q_b, k_b, v_b]
    conv_phase(nc, "pos", True, x, pos_w.rearrange("a b o c -> a b (o c)"), pos_b, None, x1_d, xr_d, xc_d)
    attention_phase(nc, "rows", True, xr_d, mask_w, *qkv, ln1_g, ln1_b, v_d, row_d)
    attention_phase(nc, "cols", False, xc_d, mask_h, *qkv, ln1_g, ln1_b, row_d, att_d)
    conv_phase(nc, "lepe", False, v_d, lepe_w.rearrange("a b o c -> a b (o c)"), lepe_b, att_d,
               None, rt_d, None)
    mlp_phase(nc, "mlp", rt_d, x1_d, out_w, out_b, ln2_g, ln2_b, fc1_w, fc1_b, fc2_w, fc2_b, out)


_INS = ["x"] + ["L0_conv_" + n for n in (
    "mask_h", "mask_w", "pos_w", "pos_b", "ln1_g", "ln1_b", "q_w", "q_b", "k_w", "k_b", "v_w", "v_b", "lepe_w",
    "lepe_b", "out_w", "out_b", "ln2_g", "ln2_b", "fc1_w", "fc1_b", "fc2_w", "fc2_b")]
_OUTS = [((B, H, W, C), "float32")]


def kernel(**inputs):
    import numpy as _np
    import concourse.bacc as _bacc
    from concourse import mybir as _mybir
    from concourse.bass_utils import run_bass_kernel_spmd as _run

    nc = _bacc.Bacc("TRN2", target_bir_lowering=False, num_devices=1)
    arrays, args = {}, []
    for name in _INS:
        a = _np.ascontiguousarray(inputs[name])
        arrays[f"in_{name}_dram"] = a
        args.append(nc.dram_tensor(f"in_{name}_dram", a.shape, _mybir.dt.from_np(a.dtype), kind="ExternalInput").ap())
    for i, (shape, dtype) in enumerate(_OUTS):
        dt = _mybir.dt.from_np(_np.dtype(dtype))
        args.append(nc.dram_tensor(f"out_{i}_dram", shape, dt, kind="ExternalOutput").ap())
    build(nc, *args)
    r = _run(nc, [arrays], core_ids=[0])
    got = tuple(r.results[0][f"out_{i}_dram"] for i in range(len(_OUTS)))
    return got[0]
```
